# Optimizing a Trainium2 kernel written in Bass

```python
import numpy as np
import jax
import jax.numpy as jnp

def _softmax(x, axis=-1):
    return jax.nn.softmax(x, axis=axis)

def _gelu(x):
    return jax.nn.gelu(x, approximate=True)

def _silu(x):
    return jax.nn.silu(x)

def _sigmoid(x):
    return jax.nn.sigmoid(x)

def _layernorm(x, axis=-1, eps=1e-05):
    m = jnp.mean(x, axis=axis, keepdims=True)
    v = jnp.var(x, axis=axis, keepdims=True)
    return (x - m) / jnp.sqrt(v + eps)

def _scatter_add(tgt, idx, src, axis=0):
    return tgt.at[idx].add(src)

def _segment_sum(src, seg, n):
    return jax.ops.segment_sum(src, seg, n)
kernel_name = 'mk_adj_preln_d2_adj_r2_92efcc'

def setup_inputs(seed: int=0):
    np.random.seed(seed)
    _w = jnp.asarray

    def _rec_inputs():
        import jax
        import jax.numpy as jnp
        _gk = jax.random.key(seed)
        x = -0.0001538 + 1 * jax.random.normal(jax.random.fold_in(_gk, 1), (32, 256, 384), jnp.float32)
        _a = jax.random.bernoulli(jax.random.fold_in(_gk, 2), 0.0078125, (32, 256, 256))
        _a = jnp.logical_or(_a, jnp.swapaxes(_a, -1, -2))
        _a = jnp.logical_or(_a, jnp.eye(256, dtype=bool))
        adj = _a
        return (x, adj)
    x, adj = _rec_inputs()

    def _L0_gnn_setup():
        import jax, jax.numpy as jnp
        import numpy as np
        B, S, H = (4, 1024, 384)
        NUM_HEADS = 6
        HEAD_SIZE = H // NUM_HEADS
        NEG = -9000000000000000.0

        def _heads(x):
            b, s, _ = x.shape
            return x.reshape(b, s, NUM_HEADS, HEAD_SIZE).transpose(0, 2, 1, 3)
        key = jax.random.key(seed)
        ks = jax.random.split(key, 10)
        seq_inputs = jax.random.normal(ks[0], (B, S, H), dtype=jnp.float32)
        gm = jax.random.randint(ks[1], (B, S, S), 0, 2) > 0
        graph_mask = gm | jnp.eye(S, dtype=bool)[None]
        sc = 1.0 / np.sqrt(H)
        Wq = jax.random.normal(ks[2], (H, H), dtype=jnp.float32) * sc
        bq = jnp.zeros((H,), dtype=jnp.float32)
        Wk = jax.random.normal(ks[3], (H, H), dtype=jnp.float32) * sc
        bk = jnp.zeros((H,), dtype=jnp.float32)
        Wv = jax.random.normal(ks[4], (H, H), dtype=jnp.float32) * sc
        bv = jnp.zeros((H,), dtype=jnp.float32)
        Wf = jax.random.normal(ks[5], (H, H), dtype=jnp.float32) * sc
        bf = jnp.zeros((H,), dtype=jnp.float32)
        return {'seq_inputs': seq_inputs, 'Wq': Wq, 'bq': bq, 'Wk': Wk, 'bk': bk, 'Wv': Wv, 'bv': bv, 'Wf': Wf, 'bf': bf, 'graph_mask': graph_mask}
    _L0_gnn_all = _L0_gnn_setup()
    _L0_gnn_in = {k: v for k, v in _L0_gnn_all.items() if k in ('Wq', 'bq', 'Wk', 'bk', 'Wv', 'bv', 'Wf', 'bf')}
    del _L0_gnn_all

    def _L1_gnn_setup():
        import jax, jax.numpy as jnp
        import numpy as np
        ATT_HEAD = 12
        IN_DIM = 384
        OUT_DIM = IN_DIM // ATT_HEAD
        LEAKY_ALPHA = 0.2
        B, N = (8, 256)
        key = jax.random.key(seed)
        ks = jax.random.split(key, 8)
        feat_in = jax.random.normal(ks[0], (B, N, IN_DIM), dtype=jnp.float32)
        adj = jax.random.randint(ks[1], (B, N, N), 0, 2) > 0
        lim_W = float(np.sqrt(6.0 / (IN_DIM + OUT_DIM)))
        W = jax.random.uniform(ks[2], (ATT_HEAD, IN_DIM, OUT_DIM), minval=-lim_W, maxval=lim_W, dtype=jnp.float32)
        b = jnp.zeros((OUT_DIM,), dtype=jnp.float32)
        lim_w = float(np.sqrt(6.0 / (OUT_DIM + 1)))
        w_src = jax.random.uniform(ks[3], (ATT_HEAD, OUT_DIM, 1), minval=-lim_w, maxval=lim_w, dtype=jnp.float32)
        w_dst = jax.random.uniform(ks[4], (ATT_HEAD, OUT_DIM, 1), minval=-lim_w, maxval=lim_w, dtype=jnp.float32)
        std_H = float(np.sqrt(2.0 / (IN_DIM + IN_DIM)))
        H_w = jax.random.normal(ks[5], (IN_DIM, IN_DIM), dtype=jnp.float32) * std_H
        H_b = jax.random.normal(ks[6], (IN_DIM,), dtype=jnp.float32) * 0.01
        return {'feat_in': feat_in, 'adj': adj, 'W': W, 'b': b, 'w_src': w_src, 'w_dst': w_dst, 'H_w': H_w, 'H_b': H_b}
    _L1_gnn_all = _L1_gnn_setup()
    _L1_gnn_in = {k: v for k, v in _L1_gnn_all.items() if k in ('W', 'b', 'w_src', 'w_dst', 'H_w', 'H_b')}
    del _L1_gnn_all
    return {'x': x, 'adj': adj, 'L0_gnn_Wq': _L0_gnn_in['Wq'], 'L0_gnn_bq': _L0_gnn_in['bq'], 'L0_gnn_Wk': _L0_gnn_in['Wk'], 'L0_gnn_bk': _L0_gnn_in['bk'], 'L0_gnn_Wv': _L0_gnn_in['Wv'], 'L0_gnn_bv': _L0_gnn_in['bv'], 'L0_gnn_Wf': _L0_gnn_in['Wf'], 'L0_gnn_bf': _L0_gnn_in['bf'], 'L1_gnn_W': _L1_gnn_in['W'], 'L1_gnn_b': _L1_gnn_in['b'], 'L1_gnn_w_src': _L1_gnn_in['w_src'], 'L1_gnn_w_dst': _L1_gnn_in['w_dst'], 'L1_gnn_H_w': _L1_gnn_in['H_w'], 'L1_gnn_H_b': _L1_gnn_in['H_b']}

def reference(x, adj, L0_gnn_Wq, L0_gnn_bq, L0_gnn_Wk, L0_gnn_bk, L0_gnn_Wv, L0_gnn_bv, L0_gnn_Wf, L0_gnn_bf, L1_gnn_W, L1_gnn_b, L1_gnn_w_src, L1_gnn_w_dst, L1_gnn_H_w, L1_gnn_H_b):
    import jax
    import jax.numpy as jnp

    def _L0_gnn_ref(seq_inputs, Wq, bq, Wk, bk, Wv, bv, Wf, bf, graph_mask):
        import jax, jax.numpy as jnp
        import numpy as np
        B, S, H = (4, 1024, 384)
        NUM_HEADS = 6
        HEAD_SIZE = H // NUM_HEADS
        NEG = -9000000000000000.0

        def _heads(x):
            b, s, _ = x.shape
            return x.reshape(b, s, NUM_HEADS, HEAD_SIZE).transpose(0, 2, 1, 3)
        q = _heads(seq_inputs @ Wq + bq)
        k = _heads(seq_inputs @ Wk + bk)
        v = _heads(seq_inputs @ Wv + bv)
        scores = jnp.einsum('bhqd,bhkd->bhqk', q, k) / np.sqrt(HEAD_SIZE)
        bias = jnp.where(graph_mask, 0.0, NEG)[:, None]
        probs = jax.nn.softmax(scores + bias, axis=-1)
        ctx = jnp.einsum('bhqk,bhkd->bhqd', probs, v)
        ctx = ctx.transpose(0, 2, 1, 3).reshape(seq_inputs.shape[0], seq_inputs.shape[1], H)
        return ctx @ Wf + bf

    def _L1_gnn_ref(feat_in, adj, W, b, w_src, w_dst, H_w, H_b):
        import jax, jax.numpy as jnp
        import numpy as np
        ATT_HEAD = 12
        IN_DIM = 384
        OUT_DIM = IN_DIM // ATT_HEAD
        LEAKY_ALPHA = 0.2
        B, N = (8, 256)
        h = jnp.einsum('bnd,ade->bane', feat_in, W)
        th = jnp.tanh(h)
        attn_src = jnp.einsum('bane,aeo->bano', th, w_src)
        attn_dst = jnp.einsum('bane,aeo->bano', th, w_dst)
        attn = attn_src + jnp.swapaxes(attn_dst, 2, 3)
        attn = jnp.where(attn >= 0, attn, LEAKY_ALPHA * attn)
        mask = ~adj[:, None, :, :]
        attn = jnp.where(mask, jnp.float32(-999.0), attn)
        attn = jax.nn.softmax(attn, axis=-1)
        feat_out = jnp.einsum('banm,bame->bane', attn, h) + b
        feat_out = jnp.swapaxes(feat_out, 1, 2).reshape(feat_in.shape[0], feat_in.shape[1], -1)
        feat_out = jax.nn.elu(feat_out)
        gate = jax.nn.sigmoid(feat_in @ H_w.T + H_b)
        return gate * feat_out + (1.0 - gate) * feat_in
    h = jnp.maximum(_layernorm(x, axis=-1), 0.0)
    x = x + _L0_gnn_ref(h, L0_gnn_Wq, L0_gnn_bq, L0_gnn_Wk, L0_gnn_bk, L0_gnn_Wv, L0_gnn_bv, L0_gnn_Wf, L0_gnn_bf, adj)
    h = jnp.maximum(_layernorm(x, axis=-1), 0.0)
    x = x + _L1_gnn_ref(h, adj, L1_gnn_W, L1_gnn_b, L1_gnn_w_src, L1_gnn_w_dst, L1_gnn_H_w, L1_gnn_H_b)
    return x

_drawn_inputs = setup_inputs


def setup_inputs(seed=0):
    import zlib

    import numpy as np

    out = dict(_drawn_inputs(seed))
    spreads = {'L0_gnn_bq': (0.0, 0.673),
     'L0_gnn_bk': (0.0, 2.0),
     'L0_gnn_bv': (0.0, 0.1),
     'L0_gnn_bf': (0.0, 0.1),
     'L1_gnn_b': (0.0, 0.1)}
    factors = {'L1_gnn_w_src': 11.142, 'L1_gnn_H_b': 37.84}
    for name, (base, spread) in spreads.items():
        noise = np.random.default_rng([zlib.crc32(name.encode()), seed]).standard_normal(out[name].shape)
        drawn = base * np.exp(spread * noise) if base else spread * noise
        out[name] = jnp.asarray(drawn.astype(out[name].dtype))
    for name, factor in factors.items():
        out[name] = (out[name] * factor).astype(out[name].dtype)
    return out
```

```python
import concourse.bass as bass
from concourse import mybir

F32 = mybir.dt.float32
F32R = mybir.dt.float32r
BF16 = mybir.dt.bfloat16
U8 = mybir.dt.uint8
ALU = mybir.AluOpType
ACT = mybir.ActivationFunctionType
AX = mybir.AxisListType

P = 128
GRAPHS, NODES, H = 32, 256, 384
PAIRS = GRAPHS // 2
T = 2 * NODES // P
W = T * P
KC = H // P
NH, HD = 6, 64
AH, OD = 12, 32
E1 = OD + 1
UNITS = 2 * NH
SLOTS = 10
PROJECTIONS = [("Q", c) for c in range(KC)] + [("K", c) for c in range(KC)] + [("V", t) for t in range(T)]
STEPS = 15
FIRST = 7
EPS = 1e-5
MASKED = -9000000000000000.0
LEAK = 0.2
SHIFT = 40.0

def unit(n):
    c, g, side = n // 4, (n // 2) % 2, n % 2
    return c, g, side, 2 * c + side


class Signal:

    def __init__(self, nc, name, per):
        self.sem, self.per = nc.alloc_semaphore(name), per

    def upto(self, p, k):
        return p * self.per + k


def due(p, k):
    return not isinstance(p, int) or p > 0 or (p == 0 and k > 0)


class Chain:

    def __init__(self, nc, name):
        self.sem, self.per, self.count = nc.alloc_semaphore(name), None, 0

    def start(self, p):
        if self.per is None and self.count:
            self.per = self.count
        assert isinstance(p, int) and p == 0 or self.per is not None
        self.count = 0

    def link(self, eng, ins, p):
        self.count += 1
        ins.then_inc(self.sem, 1)
        eng.wait_ge(self.sem, (0 if isinstance(p, int) and p == 0 else p * self.per) + self.count)


def _banks():
    layer0 = [("A", c) for c in range(KC)] + [("Q", c) for c in range(KC)] + [("K", c) for c in range(KC)]
    layer0 += [("V", t) for t in range(T)]
    for s in range(UNITS + 1):
        layer0 += [("S", s)] * (s < UNITS) + [("PT", s - 1)] * (s >= 1)
    layer0 += [("D", t) for t in range(T)]
    layer0 = [(x, n % 3) for n, x in enumerate(layer0)]
    layer1 = [("E", c) for c in range(KC)]
    for t in range(T):
        layer1 += [("h", t), ("gate", t)]
    layer1 += [("sT", 0)]
    layer1 = [(x, 4 + n % 4) for n, x in enumerate(layer1)]
    layer1 += [(("SR", n), 4 + n % 2) for n in range(UNITS)]
    uses = {}
    for lot in (layer0, layer1):
        last = {}
        for n, (x, b) in enumerate(lot):
            uses[x] = (b, n, last.get(b))
            last[b] = x
        for x, (b, n, before) in list(uses.items()):
            if before is None:
                uses[x] = (b, n, (last.get(b), "pair before"))
    return uses, len(layer0), len(layer1)


USES, USES0, USES1 = _banks()


def graph_layers(nc, x, adj, adjT, Wq, Wk, Wv, Wf, W1, HwT, bq, bk, bv, bf, gb, w_src, w_dst, Hb, out):
    x_v = x.rearrange("(a g) (c q) f -> a q (g c) f", g=2, q=P)
    adj_v = adj.rearrange("(a g) (c q) k -> a q (g c) k", g=2, q=P)
    adjT_v = adjT.rearrange("(a g) (c q) k -> a q (g c) k", g=2, q=P)
    out_v = out.rearrange("(a g) (c q) f -> a q (g c) f", g=2, q=P)

    def sb(name, shape, dt=F32):
        return nc.alloc_sbuf_tensor(name, shape, dt)

    w_names = ("Wq", "Wk", "Wv", "Wf", "W1", "Hw")
    w_dram = (Wq, Wk, Wv, Wf, W1, HwT)
    w_hi = {n: sb(n + "_hi", [P, KC, H], F32R) for n in w_names}
    w_lo = {n: sb(n + "_lo", [P, KC, H], F32R) for n in w_names}
    bv_b, bf_b, Hb_b = sb("bv_b", [P, H]), sb("bf_b", [P, H]), sb("Hb_b", [P, H])
    wsrc_b, wdst_b, gb_b = sb("wsrc_b", [P, H]), sb("wdst_b", [P, H]), sb("gb_b", [P, OD])
    bq_c, bk_c = sb("bq_c", [P, KC]), sb("bk_c", [P, KC])
    ident = sb("ident", [P, P])
    ident_b = sb("ident_b", [P, P], BF16)
    sel = sb("sel", [P, AH, P], BF16)
    half = sb("half", [P, 2 * T])
    x_sb, xb = sb("x_sb", [P, T, H]), sb("xb", [P, T, H])
    adj_u = sb("adj_u", [P, T, NODES], U8)
    mask = sb("mask", [P, T, NODES], BF16)
    stats, mv, rstd, veps = sb("stats", [P, T, 6]), sb("mv", [P, T, 2]), sb("rstd", [P, T]), sb("veps", [P, T])
    hn = sb("hn", [P, T, H])
    hT_hi, hT_lo = sb("hT_hi", [P, KC, W], F32R), sb("hT_lo", [P, KC, W], F32R)
    qz, kT, v_sb = sb("qz", [P, NH, W]), sb("kT", [P, KC, W]), sb("v_sb", [P, T, H])
    probs = sb("probs", [P, 2, 2, NODES])
    probsT = sb("probsT", [P, 2, 2, NODES])
    nmax, rsum, rinv = sb("nmax", [P, 4, 2]), sb("rsum", [P, 4, 2]), sb("rinv", [P, 4, 2])
    y = sb("y", [P, T, H])
    adjT_u = sb("adjT_u", [P, T, NODES], U8)
    adj_p, adj_n = sb("adj_p", [P, T, NODES], BF16), sb("adj_n", [P, T, NODES], BF16)
    stats2, mv2, rstd2, veps2 = sb("stats2", [P, T, 6]), sb("mv2", [P, T, 2]), sb("rstd2", [P, T]), sb("veps2", [P, T])
    hr, hy = sb("hr", [P, T, H]), sb("hy", [P, T, H])
    h1 = sb("h1", [P, T, AH, OD])
    gl = sb("gl", [P, T, H])
    sd = sb("sd", [P, T, 2 * AH])
    dmax2, dmax = sb("dmax2", [P, 2 * AH]), sb("dmax", [P, 2 * AH])
    s_rest = sb("s_rest", [P, T, AH])
    s_parts = sb("s_parts", [P, T, 3 * AH], BF16)
    sT = sb("sT", [P, W], BF16)
    d_neg = sb("d_neg", [P, T, AH])
    u_sb, m_sb = sb("u_sb", [P, T, AH]), sb("m_sb", [P, T, AH])
    e_in, e_out = sb("e_in", [P, T, 3, AH]), sb("e_out", [P, T, 3, AH])
    e_leak = sb("e_leak", [P, T, AH])
    a_neg = sb("a_neg", [P, T, AH])
    G = sb("G", [P, 2, 2, AH, E1])
    g_flat = G[:, :, :, :, :].rearrange("p s r h e -> p (s r h e)")
    tw = g_flat[:, 0:4 * H].rearrange("p (s h e) -> p s h e", s=2, e=OD)
    stage = g_flat[:, 0:KC * H].rearrange("p (c n) -> p c n", c=KC)
    X = sb("X", [P, T, 3, 2, AH, E1], BF16)
    Mp = sb("Mp", [P, 2, 2, 2, NODES], BF16)
    part1, part2 = sb("part1", [P, 2, NH, E1]), sb("part2", [P, 2, NH, E1])
    dinv = sb("dinv", [P, 2, NH])
    e_sb = sb("e_sb", [P, 2, H])
    th = e_sb[:, :, :].rearrange("p s (h e) -> p s h e", e=OD)
    cT_hi, cT_lo = hT_hi, hT_lo

    bank = [nc.alloc_psum_tensor(f"bank{b}", [P, 512], F32) for b in range(8)]
    ctx = bank[3]
    acc = [bank[6], bank[7]]

    def sig(name, per):
        return Signal(nc, name, per)

    w_in, w_hi_done, w_lo_done = sig("w_in", 0), sig("w_hi_done", 0), sig("w_lo_done", 0)
    rows_in, consts = sig("rows_in", 0), sig("consts", 0)
    x_in, adj_in, adjT_in = sig("x_in", 16), sig("adj_in", 16), sig("adjT_in", 16)
    use0, use1 = sig("use0", USES0), sig("use1", USES1)
    stat_done, rstd_done, ln1_done = sig("stat_done", 1), sig("rstd_done", 1), sig("ln1_done", T)
    xb_done, mask_done = sig("xb_done", 1), sig("mask_done", 1)
    hi_done, lo_done = sig("hi_done", KC), sig("lo_done", KC)
    q_done, k_done, v_done = sig("q_done", NH), sig("k_done", KC), sig("v_done", T)
    max_done, exp_done, rinv_done = sig("max_done", UNITS), sig("exp_done", 2 * UNITS), sig("rinv_done", UNITS)
    pn_done, pt_done, pv_done = sig("pn_done", 2 * UNITS), sig("pt_done", UNITS), sig("pv_done", UNITS)
    chi_done, clo_done, y_done = sig("chi_done", KC), sig("clo_done", KC), sig("y_done", T)
    adjT_done, adjN_done = sig("adjT_done", 1), sig("adjN_done", 1)
    stat2_done, rstd2_done, ln2_done = sig("stat2_done", 1), sig("rstd2_done", 1), sig("ln2_done", T)
    hr_done, hy_done = sig("hr_done", T), sig("hy_done", T)
    hi2_done, lo2_done = sig("hi2_done", KC), sig("lo2_done", KC)
    th_done, h1_done, gl_done, gate_done = sig("th_done", T), sig("h1_done", T), sig("gl_done", T), sig("gate_done", T)
    tw_done, sd_done, dm_done, dmax_done = sig("tw_done", T), sig("sd_done", T), sig("dm_done", 1), sig("dmax_done", 1)
    parts_done, sT_done = sig("parts_done", 1), sig("sT_done", 1)
    ein_done, e_done, dneg_done, aneg_done = sig("ein_done", 1), sig("e_done", 2), sig("dneg_done", 1), sig("aneg_done", 1)
    g1_done, g2_done = sig("g1_done", T), sig("g2_done", T)
    x0_done, r_done, x1_done, x2_done = sig("x0_done", T), sig("r_done", T), sig("x1_done", T), sig("x2_done", T)
    m_done, mm_done = sig("m_done", UNITS), sig("mm_done", UNITS)
    acc_out, num_done, f_done, v1_done = sig("acc_out", 2 * T), sig("num_done", 2 * T), sig("f_done", 2 * T), sig("v1_done", T)
    e1_done, elu_done, w1_done, out_done, stored = (sig("e1_done", T), sig("elu_done", T), sig("w1_done", T),
                                                   sig("out_done", T), sig("stored", 16 * T))
    chain_d0, chain_d1 = Chain(nc, "chain_d0"), Chain(nc, "chain_d1")
    chain_p0, chain_p1 = Chain(nc, "chain_p0"), Chain(nc, "chain_p1")
    chain_a2, chain_d2 = Chain(nc, "chain_a2"), Chain(nc, "chain_d2")

    def bank_of(name, k):
        return bank[USES[name, k][0]]

    def filled(name, k):
        return USES[name, k][1] + 1

    def read(name, k):
        return {
            "A": (lo_done, k + 1), "Q": (q_done, 2 * k + 2), "K": (k_done, k + 1), "V": (v_done, k + 1),
            "S": (exp_done, 2 * k + 2), "PT": (pt_done, k + 1), "D": (y_done, k + 1),
            "E": (lo2_done, k + 1), "h": (h1_done, k + 1), "gate": (gl_done, k + 1), "sT": (sT_done, 1),
            "SR": (m_done, k + 1), "acc": (acc_out, 2 * T),
        }[name]

    def before(p, name, k):
        b, _, what = USES[name, k]
        if what[1] == "pair before":
            return (*read("acc", 0), p - 1) if name == "E" and b in (6, 7) else (*read(*what[0]), p - 1)
        return (*read(*what), p)

    def used_before(p, name, k):
        signal, count, pair = before(p, name, k)
        return due(pair, count)

    def reader_done(p, name, k):
        signal, count, pair = before(p, name, k)
        return signal.sem, signal.upto(pair, count)

    def seg(n):
        return slice(n * P, (n + 1) * P)

    def gat(n):
        return n // 6, 2 * (n % 6)

    waited = nc.alloc_semaphore("waited")

    def settle(eng):
        eng.sem_inc(waited, 1)

    def sync_body(sp, pn, p0, p1, p2):
        if pn is not None:
            if due(pn - 1, 1):
                sp.wait_ge(ln1_done.sem, ln1_done.upto(pn - 1, T))
                settle(sp)
                sp.wait_ge(xb_done.sem, xb_done.upto(pn - 1, 1))
                settle(sp)
            sp.dma_start(x_sb[:, :, :], x_v[pn, :, :, :]).then_inc(x_in.sem, 16)
            if due(pn - 1, 1):
                sp.wait_ge(mask_done.sem, mask_done.upto(pn - 1, 1))
                settle(sp)
            sp.dma_start(adj_u[:, :, :], adj_v[pn, :, :, :]).then_inc(adj_in.sem, 16)
        if p0 is not None:
            if due(p0 - 1, 2):
                sp.wait_ge(adjT_done.sem, adjT_done.upto(p0 - 1, 1))
                settle(sp)
                sp.wait_ge(adjN_done.sem, adjN_done.upto(p0 - 1, 1))
                settle(sp)
            sp.dma_start(adjT_u[:, :, :], adjT_v[p0, :, :, :]).then_inc(adjT_in.sem, 16)
        if p2 is not None:
            for t in range(T):
                sp.wait_ge(out_done.sem, out_done.upto(p2, t + 1))
                settle(sp)
                sp.dma_start(out_v[p2, :, t, :], h1[:, t, :, :].rearrange("p h e -> p (h e)")).then_inc(stored.sem, 16)

    def split_product(o, stat_hi, stat_lo, mov_hi, mov_lo):
        for c in range(KC):
            nc.tensor.matmul(o, stat_hi(c), mov_hi(c), start=c == 0, stop=False)
            nc.tensor.matmul(o, stat_hi(c), mov_lo(c), start=False, stop=False)
            last = nc.tensor.matmul(o, stat_lo(c), mov_hi(c), start=False, stop=c == KC - 1)
        return last

    def project_T(o, name, c):
        return split_product(o[:, :], lambda k: w_hi[name][:, k, seg(c)], lambda k: w_lo[name][:, k, seg(c)],
                             lambda k: hT_hi[:, k, :], lambda k: hT_lo[:, k, :])

    def project(o, name, t):
        return split_product(o[:, 0:H], lambda k: hT_hi[:, k, seg(t)], lambda k: hT_lo[:, k, seg(t)],
                             lambda k: w_hi[name][:, k, :], lambda k: w_lo[name][:, k, :])

    def tensor_body(pe, p0, p1, p2):
        def s_rows(n, p):
            g, head = gat(n)
            if used_before(p, "SR", n):
                pe.wait_ge(*reader_done(p, "SR", n))
            o = bank_of("SR", n)
            for k in range(2):
                last = nc.tensor.matmul(o[:, k * NODES:(k + 1) * NODES], sel[:, head + k, :],
                                        sT[:, g * NODES:(g + 1) * NODES], start=True, stop=True)
            last.then_inc(use1.sem, 1)

        def gather(n, p):
            g, head = gat(n)
            first = head - head % NH
            if n == 0:
                pe.wait_ge(x2_done.sem, x2_done.upto(p, T))
                pe.wait_ge(adjT_done.sem, adjT_done.upto(p, 1))
                pe.wait_ge(gl_done.sem, gl_done.upto(p, T))
                pe.wait_ge(sT_done.sem, sT_done.upto(p, 1))
            elif n % 3 == 0:
                pe.wait_ge(acc_out.sem, acc_out.upto(p, 2 * (n // 3)))
            if n % 3 == 0:
                for i in range(2):
                    for j in range(2):
                        for part in range(3):
                            nc.tensor.matmul(acc[i][:, NH * E1:2 * NH * E1], adj_p[:, 2 * g + j, seg(i)],
                                             X[:, 2 * g + j, part, 1, first:first + NH, :],
                                             start=j == 0 and part == 0, stop=False, skip_group_check=True)
            pe.wait_ge(m_done.sem, m_done.upto(p, n + 1))
            for k in range(2):
                col = (head + k) % NH
                for i in range(2):
                    o = acc[i][:, 0:2 * NH * E1].rearrange("p (r h e) -> p r h e", r=2, h=NH)[:, :, col, :]
                    for j in range(2):
                        for part in range(3):
                            last = nc.tensor.matmul(o, Mp[:, n % 2, k, j, seg(i)], X[:, 2 * g + j, part, :, head + k, :],
                                                    start=False, stop=False, skip_group_check=True)
            last.then_inc(mm_done.sem, 1)

        def scores(n):
            c, g, side, head = unit(n)
            if used_before(p0, "S", n):
                pe.wait_ge(*reader_done(p0, "S", n))
            o = bank_of("S", n)
            pe.wait_ge(q_done.sem, q_done.upto(p0, head + 1))
            pe.wait_ge(k_done.sem, k_done.upto(p0, c + 1))
            if n == 0:
                pe.wait_ge(mask_done.sem, mask_done.upto(p0, 1))
            for q in range(2):
                t = 2 * g + q
                o_q = o[:, q * NODES:(q + 1) * NODES]
                nc.tensor.matmul(o_q, qz[:, head, seg(t)], kT[:, c, g * NODES:(g + 1) * NODES], start=True, stop=False)
                last = nc.tensor.matmul(o_q, ident_b[:, :], mask[:, t, :], start=False, stop=True)
            last.then_inc(use0.sem, 1)

        def probs_T(n):
            if used_before(p0, "PT", n):
                pe.wait_ge(*reader_done(p0, "PT", n))
            o = bank_of("PT", n)
            for q in range(2):
                pe.wait_ge(pn_done.sem, pn_done.upto(p0, 2 * n + q + 1))
                for k in range(2):
                    last = nc.tensor.transpose(o[:, k * NODES + q * P:k * NODES + (q + 1) * P],
                                               probs[:, n % 2, q, seg(k)], ident[:, :])
            last.then_inc(use0.sem, 1)

        def context(n):
            c, g, side, head = unit(n)
            pe.wait_ge(pt_done.sem, pt_done.upto(p0, n + 1))
            if n == 0:
                pe.wait_ge(v_done.sem, v_done.upto(p0, T))
            if n == 0 and due(p0 - 1, KC):
                pe.wait_ge(clo_done.sem, clo_done.upto(p0 - 1, KC))
            if n % 4 == 0 and c > 0:
                pe.wait_ge(clo_done.sem, clo_done.upto(p0, c))
            for k in range(2):
                last = nc.tensor.matmul(ctx[side * HD:(side + 1) * HD, g * NODES:(g + 1) * NODES],
                                        v_sb[:, 2 * g + k, head * HD:(head + 1) * HD], probsT[:, n % 2, k, :],
                                        start=k == 0, stop=k == 1)
            last.then_inc(pv_done.sem, 1)

        if p0 is not None:
            for c in range(KC):
                if used_before(p0, "A", c):
                    pe.wait_ge(*reader_done(p0, "A", c))
                o = bank_of("A", c)
                for t in range(T):
                    if c == 0:
                        pe.wait_ge(ln1_done.sem, ln1_done.upto(p0, t + 1))
                    last = nc.tensor.transpose(o[:, seg(t)], hn[:, t, seg(c)], ident[:, :])
                last.then_inc(use0.sem, 1)
        for slot in range(SLOTS):
            if p2 is not None and slot < 6:
                s_rows(6 + slot, p2)
            if p0 is not None and slot == 0:
                pe.wait_ge(hi_done.sem, hi_done.upto(p0, KC))
                pe.wait_ge(lo_done.sem, lo_done.upto(p0, KC))
            if p0 is not None:
                what, k = PROJECTIONS[slot]
                if used_before(p0, what, k):
                    pe.wait_ge(*reader_done(p0, what, k))
                o = bank_of(what, k)
                if what == "V":
                    project(o, "Wv", k).then_inc(use0.sem, 1)
                else:
                    project_T(o, {"Q": "Wq", "K": "Wk"}[what], k).then_inc(use0.sem, 1)
            if p2 is not None and slot < 6:
                gather(6 + slot, p2)
        if p1 is not None:
            for c in range(KC):
                if used_before(p1, "E", c):
                    pe.wait_ge(*reader_done(p1, "E", c))
                o = bank_of("E", c)
                for t in range(T):
                    if c == 0:
                        pe.wait_ge(ln2_done.sem, ln2_done.upto(p1, t + 1))
                    last = nc.tensor.transpose(o[:, seg(t)], hn[:, t, seg(c)], ident[:, :])
                last.then_inc(use1.sem, 1)
            pe.wait_ge(hi2_done.sem, hi2_done.upto(p1, KC))
            pe.wait_ge(lo2_done.sem, lo2_done.upto(p1, KC))
            for t in range(T):
                for what, name in (("h", "W1"), ("gate", "Hw")):
                    if used_before(p1, what, t):
                        pe.wait_ge(*reader_done(p1, what, t))
                    project(bank_of(what, t), name, t).then_inc(use1.sem, 1)
        for s in range(STEPS):
            if p0 is not None and s < UNITS:
                scores(s)
            if p1 is not None and s == FIRST:
                if used_before(p1, "sT", 0):
                    pe.wait_ge(*reader_done(p1, "sT", 0))
                pe.wait_ge(parts_done.sem, parts_done.upto(p1, 1))
                settle(pe)
                o_b = bank_of("sT", 0)[:, :].bitcast(BF16)
                for t in range(T):
                    last = nc.tensor.transpose(o_b[0:3 * AH, seg(t)], s_parts[:, t, :], ident_b[:, :])
                last.then_inc(use1.sem, 1)
            if p0 is not None and 0 <= s - 1 < UNITS:
                probs_T(s - 1)
            if p1 is not None and s == FIRST:
                pe.wait_ge(sT_done.sem, sT_done.upto(p1, 1))
            if p1 is not None and 0 <= s - FIRST < 6:
                s_rows(s - FIRST, p1)
            if p1 is not None and 0 <= s - FIRST - 1 < 6:
                gather(s - FIRST - 1, p1)
            if p0 is not None and 0 <= s - 2 < UNITS:
                context(s - 2)
            if p0 is not None and s == UNITS + 2:
                pe.wait_ge(chi_done.sem, chi_done.upto(p0, KC))
                pe.wait_ge(clo_done.sem, clo_done.upto(p0, KC))
                for t in range(T):
                    if used_before(p0, "D", t):
                        pe.wait_ge(*reader_done(p0, "D", t))
                    project(bank_of("D", t), "Wf", t).then_inc(use0.sem, 1)

    def vector_body(dve, pn, p0, p1, p2):
        by_graph = "p (g c) h -> p g c h"
        s_of = sd[:, :, 0:AH]
        d_of = sd[:, :, AH:2 * AH]
        d4 = d_of.rearrange(by_graph, c=2)
        D4 = dmax[:, :].rearrange("p (g h) -> p g h", g=2).unsqueeze(2).broadcast_to([P, 2, 2, AH])
        if pn is not None:
            chain_d0.start(pn)
        if p1 is not None:
            chain_d1.start(p1)
        if p2 is not None:
            chain_d2.start(p2)

        def neighbours(n, p):
            g, head = gat(n)
            dve.wait_ge(use1.sem, use1.upto(p, filled("SR", n)))
            if n >= 2:
                dve.wait_ge(mm_done.sem, mm_done.upto(p, n - 1))
            elif due(p - 1, UNITS):
                dve.wait_ge(mm_done.sem, mm_done.upto(p - 1, UNITS))
            o = bank_of("SR", n)
            for k in range(2):
                for j in range(2):
                    t = 2 * g + j
                    last = nc.vector.scalar_tensor_tensor(
                        Mp[:, n % 2, k, j, :], o[:, k * NODES:(k + 1) * NODES], d_neg[:, t, head + k:head + k + 1],
                        adj_n[:, t, :], ALU.is_ge, ALU.mult)
            last.then_inc(m_done.sem, 1)

        def acc_leave(q, p):
            g, hf = q // 2, q % 2
            heads = slice(hf * NH, (hf + 1) * NH)
            dve.wait_ge(mm_done.sem, mm_done.upto(p, 3 * q + 3))
            for i in range(2):
                t = 2 * g + i
                left, right = acc[i][:, 0:NH * E1], acc[i][:, NH * E1:2 * NH * E1]
                nc.vector.tensor_tensor(part1[:, i, :, :], left.rearrange("p (h e) -> p h e", h=NH),
                                        a_neg[:, t, heads].unsqueeze(2).broadcast_to([P, NH, E1]), ALU.mult)
                nc.vector.tensor_tensor(part2[:, i, :, :], right.rearrange("p (h e) -> p h e", h=NH),
                                        e_out[:, t, 1, heads].unsqueeze(2).broadcast_to([P, NH, E1]),
                                        ALU.mult).then_inc(acc_out.sem, 1)

        def divide(q, p, chain):
            g, hf = q // 2, q % 2
            heads = slice(hf * NH, (hf + 1) * NH)
            for i in range(2):
                dve.wait_ge(num_done.sem, num_done.upto(p, 2 * q + i + 1))
                last = nc.vector.reciprocal(dinv[:, i, :], part1[:, i, :, OD])
            chain.link(dve, last, p)
            for i in range(2):
                nc.vector.tensor_tensor(h1[:, 2 * g + i, heads, :], part1[:, i, :, 0:OD],
                                        dinv[:, i, :].unsqueeze(2).broadcast_to([P, NH, OD]),
                                        ALU.mult).then_inc(f_done.sem, 1)

        def elu(t):
            dve.wait_ge(e1_done.sem, e1_done.upto(p2, t + 1))
            v = h1[:, t, :, :].rearrange("p h e -> p (h e)")
            nc.vector.scalar_tensor_tensor(v, e_sb[:, t % 2, :], -1.0, v, ALU.add, ALU.max).then_inc(elu_done.sem, 1)

        def mix(t):
            dve.wait_ge(w1_done.sem, w1_done.upto(p2, t + 1))
            dve.wait_ge(gate_done.sem, gate_done.upto(p2, t + 1))
            v = h1[:, t, :, :].rearrange("p h e -> p (h e)")
            chain_d2.link(dve, nc.vector.scalar_tensor_tensor(v, gl[:, t, :], 1.0, v, ALU.add, ALU.mult), p2)
            nc.vector.scalar_tensor_tensor(v, v, 0.5, hy[:, t, :], ALU.mult, ALU.add).then_inc(out_done.sem, 1)

        if p0 is not None:
            for c in range(KC):
                dve.wait_ge(use0.sem, use0.upto(p0, filled("A", c)))
                o = bank_of("A", c)
                dve.wait_ge(hi_done.sem, hi_done.upto(p0, c + 1))
                nc.vector.scalar_tensor_tensor(hT_lo[:, c, :], o[:, :], 0.0, hT_hi[:, c, :].bitcast(F32),
                                               ALU.max, ALU.subtract).then_inc(lo_done.sem, 1)
        for slot in range(SLOTS + 1):
            if p2 is not None and slot < 6:
                neighbours(6 + slot, p2)
            if p1 is not None and slot == 0:
                dve.wait_ge(y_done.sem, y_done.upto(p1, T))
                for t in range(T):
                    last = nc.vector.bn_stats(stats2[:, t, :], y[:, t, :])
                chain_d1.link(dve, last, p1)
                settle(dve)
                for t in range(T):
                    last = nc.vector.bn_aggr(mv2[:, t, :], stats2[:, t, :])
                last.then_inc(stat2_done.sem, 1)
            if p1 is not None and slot == 1:
                dve.wait_ge(stat2_done.sem, stat2_done.upto(p1, 1))
                dve.wait_ge(rstd2_done.sem, rstd2_done.upto(p1, 1))
                if p0 is not None:
                    dve.wait_ge(use0.sem, use0.upto(p0, filled("A", KC - 1)))
                for t in range(T):
                    nc.vector.tensor_scalar(hn[:, t, :], y[:, t, :], mv2[:, t, 0:1], rstd2[:, t:t + 1],
                                            ALU.subtract, ALU.mult).then_inc(ln2_done.sem, 1)
            if p0 is not None and 0 <= slot - 1 < SLOTS and PROJECTIONS[slot - 1][0] == "Q":
                c = PROJECTIONS[slot - 1][1]
                dve.wait_ge(use0.sem, use0.upto(p0, filled("Q", c)))
                o = bank_of("Q", c)
                for side in range(2):
                    rows = slice(side * HD, (side + 1) * HD)
                    nc.vector.tensor_scalar(qz[rows, 2 * c + side, :], o[rows, :], bq_c[rows, c:c + 1],
                                            float(HD) ** -0.5, ALU.add, ALU.mult).then_inc(q_done.sem, 1)
            if p0 is not None and 0 <= slot - 1 < SLOTS and PROJECTIONS[slot - 1][0] == "V":
                t = PROJECTIONS[slot - 1][1]
                dve.wait_ge(use0.sem, use0.upto(p0, filled("V", t)))
                o = bank_of("V", t)
                nc.vector.tensor_tensor(v_sb[:, t, :], o[:, 0:H], bv_b[:, :], ALU.add).then_inc(v_done.sem, 1)
            if p2 is not None:
                if slot in (2, 8):
                    elu((slot - 2) // 3)
                    elu((slot - 2) // 3 + 1)
                if slot in (3, 9):
                    mix((slot - 3) // 3)
                    mix((slot - 3) // 3 + 1)
                if slot in (3, 6):
                    acc_leave(slot // 3 + 1, p2)
                if slot in (4, 7):
                    divide((slot - 1) // 3 + 1, p2, chain_d2)
        if p1 is not None:
            for c in range(KC):
                dve.wait_ge(use1.sem, use1.upto(p1, filled("E", c)))
                o = bank_of("E", c)
                dve.wait_ge(hi2_done.sem, hi2_done.upto(p1, c + 1))
                nc.vector.scalar_tensor_tensor(hT_lo[:, c, :], o[:, :], 0.0, hT_hi[:, c, :].bitcast(F32),
                                               ALU.max, ALU.subtract).then_inc(lo2_done.sem, 1)
            dve.wait_ge(adjT_in.sem, adjT_in.upto(p1, 16))
            nc.vector.tensor_scalar(adj_n[:, :, :], adjT_u[:, :, :], -1.0, None, ALU.mult).then_inc(adjN_done.sem, 1)
            for t in range(T + 1):
                if t < T:
                    dve.wait_ge(use1.sem, use1.upto(p1, filled("gate", t)))
                    o = bank_of("gate", t)
                    nc.vector.tensor_tensor(gl[:, t, :], o[:, 0:H], Hb_b[:, :], ALU.add).then_inc(gl_done.sem, 1)
                if t > 0:
                    dve.wait_ge(tw_done.sem, tw_done.upto(p1, t))
                    nc.vector.tensor_reduce(sd[:, t - 1, :], tw[:, (t - 1) % 2, :, :], AX.X, ALU.add).then_inc(sd_done.sem, 1)
            dve.wait_ge(sd_done.sem, sd_done.upto(p1, T))
            nc.vector.tensor_tensor(dmax2[:, :].rearrange("p (g h) -> p g h", g=2), d4[:, :, 0, :],
                                    d4[:, :, 1, :], ALU.max).then_inc(dm_done.sem, 1)
        for s in range(STEPS):
            if p0 is not None and s < UNITS:
                dve.wait_ge(use0.sem, use0.upto(p0, filled("S", s)))
                o = bank_of("S", s)
                nc.vector.tensor_reduce(nmax[:, s % 4, :], o[:, :].rearrange("p (q k) -> p q k", q=2),
                                        AX.X, ALU.max, negate=True).then_inc(max_done.sem, 1)
            if p1 is not None and s == 0:
                sp3 = s_parts[:, :, :].rearrange("p t (j h) -> p t j h", j=3)
                chain_d1.link(dve, nc.vector.tensor_copy(sp3[:, :, 0, :], s_of), p1)
                chain_d1.link(dve, nc.vector.tensor_tensor(s_rest[:, :, :], s_of, sp3[:, :, 0, :], ALU.subtract), p1)
                chain_d1.link(dve, nc.vector.tensor_copy(sp3[:, :, 1, :], s_rest[:, :, :]), p1)
                nc.vector.tensor_tensor(sp3[:, :, 2, :], s_rest[:, :, :], sp3[:, :, 1, :], ALU.subtract).then_inc(parts_done.sem, 1)
                nc.vector.tensor_scalar(d_neg[:, :, :], d_of, -1.0, None, ALU.mult).then_inc(dneg_done.sem, 1)
                dve.wait_ge(dmax_done.sem, dmax_done.upto(p1, 1))
                chain_d1.link(dve, nc.vector.tensor_tensor(u_sb[:, :, :].rearrange(by_graph, c=2),
                                                           s_of.rearrange(by_graph, c=2), D4, ALU.add), p1)
                chain_d1.link(dve, nc.vector.scalar_tensor_tensor(m_sb[:, :, :], u_sb[:, :, :], LEAK, u_sb[:, :, :],
                                                                  ALU.mult, ALU.max), p1)
                nc.vector.tensor_tensor(e_in[:, :, 0, :], u_sb[:, :, :], m_sb[:, :, :], ALU.subtract)
                nc.vector.scalar_tensor_tensor(e_in[:, :, 1, :], u_sb[:, :, :], LEAK, m_sb[:, :, :], ALU.mult, ALU.subtract)
                nc.vector.tensor_tensor(e_in[:, :, 2, :].rearrange(by_graph, c=2), d4, D4, ALU.subtract).then_inc(ein_done.sem, 1)
            if p1 is not None and 0 <= s - FIRST < 6:
                if s == FIRST:
                    dve.wait_ge(dneg_done.sem, dneg_done.upto(p1, 1))
                    dve.wait_ge(adjN_done.sem, adjN_done.upto(p1, 1))
                neighbours(s - FIRST, p1)
            if p1 is not None and s == 1:
                dve.wait_ge(e_done.sem, e_done.upto(p1, 2))
                nc.vector.tensor_scalar(a_neg[:, :, :], e_out[:, :, 0, :], -1.0, None, ALU.mult).then_inc(aneg_done.sem, 1)
            if p1 is not None and 0 <= s - 1 < T:
                t = s - 1
                if t >= 2:
                    dve.wait_ge(x2_done.sem, x2_done.upto(p1, t - 1))
                dve.wait_ge(h1_done.sem, h1_done.upto(p1, t + 1))
                nc.vector.tensor_tensor(G[:, t % 2, 0, :, 0:OD], h1[:, t, :, :],
                                        e_out[:, t, 2, :].unsqueeze(2).broadcast_to([P, AH, OD]), ALU.mult)
                nc.vector.tensor_copy(G[:, t % 2, 0, :, OD:E1], e_out[:, t, 2, :].unsqueeze(2))
                nc.vector.tensor_copy(G[:, t % 2, 1, :, OD:E1], e_leak[:, t, :].unsqueeze(2)).then_inc(g1_done.sem, 1)
            if p0 is not None and s < UNITS:
                dve.wait_ge(exp_done.sem, exp_done.upto(p0, 2 * s + 2))
                nc.vector.reciprocal(rinv[:, s % 4, :], rsum[:, s % 4, :]).then_inc(rinv_done.sem, 1)
                dve.wait_ge(rinv_done.sem, rinv_done.upto(p0, s + 1))
                for q in range(2):
                    nc.vector.tensor_scalar(probs[:, s % 2, q, :], probs[:, s % 2, q, :], rinv[:, s % 4, q:q + 1], None,
                                            ALU.mult).then_inc(pn_done.sem, 1)
            if p1 is not None and 0 <= s - 2 < T:
                t = s - 2
                dve.wait_ge(x0_done.sem, x0_done.upto(p1, t + 1))
                flat = "p r h e -> p (r h e)"
                nc.vector.tensor_tensor(G[:, t % 2, :, :, :].rearrange(flat), G[:, t % 2, :, :, :].rearrange(flat),
                                        X[:, t, 0, :, :, :].rearrange(flat), ALU.subtract).then_inc(r_done.sem, 1)
            if p1 is not None and s in (FIRST + 4, FIRST + 7):
                q = (s - FIRST - 4) // 3
                if q == 0:
                    dve.wait_ge(aneg_done.sem, aneg_done.upto(p1, 1))
                acc_leave(q, p1)
                divide(q, p1, chain_d1)
            if p0 is not None and s in (5, 9, 13):
                c = (s - 5) // 4
                dve.wait_ge(pv_done.sem, pv_done.upto(p0, 4 * c + 4))
                dve.wait_ge(chi_done.sem, chi_done.upto(p0, c + 1))
                nc.vector.tensor_tensor(cT_lo[:, c, :], ctx[:, :], cT_hi[:, c, :].bitcast(F32),
                                        ALU.subtract).then_inc(clo_done.sem, 1)
            if pn is not None and s == 6:
                dve.wait_ge(x_in.sem, x_in.upto(pn, 16))
                for t in range(T):
                    last = nc.vector.bn_stats(stats[:, t, :], x_sb[:, t, :])
                chain_d0.link(dve, last, pn)
                settle(dve)
                for t in range(T):
                    last = nc.vector.bn_aggr(mv[:, t, :], stats[:, t, :])
                last.then_inc(stat_done.sem, 1)
            if pn is not None and s == 8:
                dve.wait_ge(stat_done.sem, stat_done.upto(pn, 1))
                dve.wait_ge(rstd_done.sem, rstd_done.upto(pn, 1))
                if p1 is not None:
                    dve.wait_ge(hr_done.sem, hr_done.upto(p1, T))
                if p1 is not None:
                    dve.wait_ge(use1.sem, use1.upto(p1, filled("E", KC - 1)))
                if p1 is None and p0 is not None:
                    dve.wait_ge(use0.sem, use0.upto(p0, filled("A", KC - 1)))
                for t in range(T):
                    nc.vector.tensor_scalar(hn[:, t, :], x_sb[:, t, :], mv[:, t, 0:1], rstd[:, t:t + 1],
                                            ALU.subtract, ALU.mult).then_inc(ln1_done.sem, 1)
            if p0 is not None and s == UNITS + 2:
                for t in range(T):
                    dve.wait_ge(use0.sem, use0.upto(p0, filled("D", t)))
                    o = bank_of("D", t)
                    if t == 0:
                        dve.wait_ge(xb_done.sem, xb_done.upto(p0, 1))
                    if t == 0 and due(p0 - 1, T):
                        dve.wait_ge(hy_done.sem, hy_done.upto(p0 - 1, T))
                    nc.vector.tensor_tensor(y[:, t, :], o[:, 0:H], xb[:, t, :], ALU.add).then_inc(y_done.sem, 1)

    def scalar_body(act, p0, p1, p2):
        if p2 is not None:
            chain_a2.start(p2)
        if p0 is not None:
            for c in range(KC):
                act.wait_ge(use0.sem, use0.upto(p0, filled("A", c)))
                o = bank_of("A", c)
                nc.scalar.activation(hT_hi[:, c, :], o[:, :], ACT.Relu).then_inc(hi_done.sem, 1)
        for slot in range(SLOTS + 1):
            if p0 is not None and 0 <= slot - 1 < SLOTS and PROJECTIONS[slot - 1][0] == "K":
                c = PROJECTIONS[slot - 1][1]
                act.wait_ge(use0.sem, use0.upto(p0, filled("K", c)))
                o = bank_of("K", c)
                nc.scalar.activation(kT[:, c, :], o[:, :], ACT.Identity, bias=bk_c[:, c:c + 1]).then_inc(k_done.sem, 1)
            if p2 is not None and slot in (1, 8):
                for t in ((0, 1) if slot == 1 else (2, 3)):
                    act.wait_ge(v1_done.sem, v1_done.upto(p2, t + 1))
                    if t >= 2:
                        act.wait_ge(elu_done.sem, elu_done.upto(p2, t - 1))
                    elif due(p2 - 1, T):
                        act.wait_ge(elu_done.sem, elu_done.upto(p2 - 1, T))
                    chain_a2.link(act, nc.scalar.activation(e_sb[:, t % 2, :], h1[:, t, :, :].rearrange("p h e -> p (h e)"),
                                                            ACT.Relu, scale=-1.0), p2)
                    nc.scalar.activation(e_sb[:, t % 2, :], e_sb[:, t % 2, :], ACT.Exp, scale=-1.0).then_inc(e1_done.sem, 1)
        if p1 is not None:
            for c in range(KC):
                act.wait_ge(use1.sem, use1.upto(p1, filled("E", c)))
                o = bank_of("E", c)
                nc.scalar.activation(hT_hi[:, c, :], o[:, :], ACT.Relu).then_inc(hi2_done.sem, 1)
            act.wait_ge(adjT_in.sem, adjT_in.upto(p1, 16))
            if due(p1 - 1, UNITS):
                act.wait_ge(mm_done.sem, mm_done.upto(p1 - 1, UNITS))
            nc.scalar.activation(adj_p[:, :, :], adjT_u[:, :, :], ACT.Copy).then_inc(adjT_done.sem, 1)
            for t in range(T):
                act.wait_ge(use1.sem, use1.upto(p1, filled("h", t)))
                o = bank_of("h", t)
                if t == 0 and due(p1 - 1, T):
                    act.wait_ge(elu_done.sem, elu_done.upto(p1 - 1, T))
                if t >= 2:
                    act.wait_ge(tw_done.sem, tw_done.upto(p1, t - 1))
                nc.scalar.activation(th[:, t % 2, :, :].rearrange("p h e -> p (h e)"), o[:, 0:H], ACT.Tanh).then_inc(th_done.sem, 1)
                if t == 0 and due(p1 - 1, 16 * T):
                    act.wait_ge(stored.sem, stored.upto(p1 - 1, 16 * T))
                nc.scalar.activation(h1[:, t, :, :].rearrange("p h e -> p (h e)"), o[:, 0:H], ACT.Copy).then_inc(h1_done.sem, 1)
            for t in range(T):
                act.wait_ge(gl_done.sem, gl_done.upto(p1, t + 1))
                nc.scalar.activation(gl[:, t, :], gl[:, t, :], ACT.Tanh, scale=0.5).then_inc(gate_done.sem, 1)

        flat = "p r h e -> p (r h e)"
        for s in range(STEPS):
            if p0 is not None and s < UNITS:
                o = bank_of("S", s)
                act.wait_ge(max_done.sem, max_done.upto(p0, s + 1))
                if s >= 2:
                    act.wait_ge(use0.sem, use0.upto(p0, filled("PT", s - 2)))
                elif due(p0 - 1, 1):
                    act.wait_ge(use0.sem, use0.upto(p0 - 1, filled("PT", UNITS - 1)))
                for q in range(2):
                    nc.scalar.activation(probs[:, s % 2, q, :], o[:, q * NODES:(q + 1) * NODES], ACT.Exp,
                                         bias=nmax[:, s % 4, q:q + 1],
                                         accum_out=rsum[:, s % 4, q:q + 1]).then_inc(exp_done.sem, 1)
            if p1 is not None and s == 0:
                act.wait_ge(ein_done.sem, ein_done.upto(p1, 1))
                nc.scalar.activation(e_out[:, :, 0:2, :], e_in[:, :, 0:2, :], ACT.Exp)
                nc.scalar.activation(e_out[:, :, 2, :], e_in[:, :, 2, :], ACT.Exp, bias=shift_c[:, :]).then_inc(e_done.sem, 1)
                nc.scalar.activation(e_leak[:, :, :], e_in[:, :, 2, :], ACT.Exp, scale=LEAK, bias=shift_c[:, :]).then_inc(e_done.sem, 1)
            if p0 is not None and 0 <= s - 1 < UNITS:
                n = s - 1
                act.wait_ge(use0.sem, use0.upto(p0, filled("PT", n)))
                o = bank_of("PT", n)
                if n >= 2:
                    act.wait_ge(pv_done.sem, pv_done.upto(p0, n - 1))
                elif due(p0 - 1, UNITS):
                    act.wait_ge(pv_done.sem, pv_done.upto(p0 - 1, UNITS))
                nc.scalar.activation(probsT[:, n % 2, :, :].rearrange("p k q -> p (k q)"), o[:, :], ACT.Copy).then_inc(pt_done.sem, 1)
            if p1 is not None and 0 <= s - 1 < T:
                t = s - 1
                act.wait_ge(g1_done.sem, g1_done.upto(p1, t + 1))
                act.wait_ge(g2_done.sem, g2_done.upto(p1, t + 1))
                nc.scalar.activation(X[:, t, 0, :, :, :].rearrange(flat), G[:, t % 2, :, :, :].rearrange(flat),
                                     ACT.Copy).then_inc(x0_done.sem, 1)
            if p1 is not None and 0 <= s - 2 < T:
                t = s - 2
                act.wait_ge(r_done.sem, r_done.upto(p1, t + 1))
                nc.scalar.activation(X[:, t, 1, :, :, :].rearrange(flat), G[:, t % 2, :, :, :].rearrange(flat),
                                     ACT.Copy).then_inc(x1_done.sem, 1)
            if p1 is not None and s == FIRST:
                act.wait_ge(use1.sem, use1.upto(p1, filled("sT", 0)))
                o = bank_of("sT", 0)
                nc.scalar.activation(sT[0:3 * AH, :], o[:, :].bitcast(BF16)[0:3 * AH, 0:W], ACT.Copy).then_inc(sT_done.sem, 1)
            if p0 is not None and s in (5, 9, 13):
                c = (s - 5) // 4
                act.wait_ge(pv_done.sem, pv_done.upto(p0, 4 * c + 4))
                nc.scalar.activation(cT_hi[:, c, :], ctx[:, :], ACT.Copy).then_inc(chi_done.sem, 1)

    def gpsimd_body(pool, pn, p0, p1, p2):
        flat = "p h e -> p (h e)"
        if pn is not None:
            chain_p0.start(pn)
        if p1 is not None:
            chain_p1.start(p1)

        def sum_parts(q, p):
            for i in range(2):
                pool.wait_ge(acc_out.sem, acc_out.upto(p, 2 * q + i + 1))
                nc.gpsimd.tensor_tensor(part1[:, i, :, :].rearrange(flat), part1[:, i, :, :].rearrange(flat),
                                        part2[:, i, :, :].rearrange(flat), ALU.add).then_inc(num_done.sem, 1)
            if q % 2:
                for i in range(2):
                    t = q - 1 + i
                    pool.wait_ge(f_done.sem, f_done.upto(p, 2 * q + i + 1))
                    nc.gpsimd.tensor_tensor(h1[:, t, :, :], h1[:, t, :, :],
                                            gb_b[:, :].unsqueeze(1).broadcast_to([P, AH, OD]), ALU.add).then_inc(v1_done.sem, 1)

        for slot in range(SLOTS + 1):
            if p1 is not None and slot == 0:
                pool.wait_ge(stat2_done.sem, stat2_done.upto(p1, 1))
                settle(pool)
                chain_p1.link(pool, nc.gpsimd.tensor_scalar(veps2[:, :], mv2[:, :, 1], EPS, None, ALU.add), p1)
                nc.gpsimd.tensor_tensor(rstd2[:, :], veps2[:, :], half[:, 0:T], ALU.pow).then_inc(rstd2_done.sem, 1)
            if p0 is not None and slot == 0:
                pool.wait_ge(adj_in.sem, adj_in.upto(p0, 16))
                if due(p0 - 1, 1):
                    pool.wait_ge(use0.sem, use0.upto(p0 - 1, filled("S", UNITS - 1)))
                settle(pool)
                nc.gpsimd.tensor_scalar(mask[:, :, :], adj_u[:, :, :], -MASKED, MASKED, ALU.mult, ALU.add).then_inc(mask_done.sem, 1)
            if p2 is not None and slot in (2, 8):
                for t in ((0, 1) if slot == 2 else (2, 3)):
                    pool.wait_ge(elu_done.sem, elu_done.upto(p2, t + 1))
                    v = h1[:, t, :, :].rearrange(flat)
                    nc.gpsimd.tensor_tensor(v, v, hr[:, t, :], ALU.subtract).then_inc(w1_done.sem, 1)
            if p2 is not None and slot in (4, 7):
                sum_parts((slot - 1) // 3 + 1, p2)
            if p0 is not None and slot == 5:
                if due(p0 - 1, T):
                    pool.wait_ge(y_done.sem, y_done.upto(p0 - 1, T))
                pool.wait_ge(x_in.sem, x_in.upto(p0, 16))
                for t in range(T):
                    last = nc.gpsimd.tensor_tensor(xb[:, t, :], x_sb[:, t, :], bf_b[:, :], ALU.add)
                last.then_inc(xb_done.sem, 1)
        if p1 is not None:
            if due(p1 - 1, T):
                pool.wait_ge(out_done.sem, out_done.upto(p1 - 1, T))
            for t in range(T):
                pool.wait_ge(ln2_done.sem, ln2_done.upto(p1, t + 1))
                settle(pool)
                nc.gpsimd.tensor_scalar(hr[:, t, :], hn[:, t, :], 0.0, None, ALU.max).then_inc(hr_done.sem, 1)
            for t in range(T):
                pool.wait_ge(th_done.sem, th_done.upto(p1, t + 1))
                if t == 0 and due(p1 - 1, T):
                    pool.wait_ge(x2_done.sem, x2_done.upto(p1 - 1, T))
                if t >= 2:
                    pool.wait_ge(sd_done.sem, sd_done.upto(p1, t - 1))
                th_f = th[:, t % 2, :, :].rearrange(flat)
                nc.gpsimd.tensor_tensor(tw[:, t % 2, 0:AH, :].rearrange(flat), th_f, wsrc_b[:, :], ALU.mult)
                nc.gpsimd.tensor_tensor(tw[:, t % 2, AH:2 * AH, :].rearrange(flat), th_f,
                                        wdst_b[:, :], ALU.mult).then_inc(tw_done.sem, 1)
            pool.wait_ge(dm_done.sem, dm_done.upto(p1, 1))
            settle(pool)
            nc.gpsimd.partition_all_reduce(dmax[:, :], dmax2[:, :], P, bass.bass_isa.ReduceOp.max).then_inc(dmax_done.sem, 1)

        for s in range(STEPS):
            if p1 is not None and 0 <= s - 1 < T:
                t = s - 1
                pool.wait_ge(e_done.sem, e_done.upto(p1, 2))
                pool.wait_ge(h1_done.sem, h1_done.upto(p1, t + 1))
                if t >= 2:
                    pool.wait_ge(x2_done.sem, x2_done.upto(p1, t - 1))
                nc.gpsimd.tensor_tensor(G[:, t % 2, 1, :, 0:OD], h1[:, t, :, :],
                                        e_leak[:, t, :].unsqueeze(2).broadcast_to([P, AH, OD]), ALU.mult).then_inc(g2_done.sem, 1)
            if p1 is not None and 0 <= s - 2 < T:
                t = s - 2
                f3 = "p r h e -> p (r h e)"
                pool.wait_ge(x1_done.sem, x1_done.upto(p1, t + 1))
                nc.gpsimd.tensor_tensor(X[:, t, 2, :, :, :].rearrange(f3), G[:, t % 2, :, :, :].rearrange(f3),
                                        X[:, t, 1, :, :, :].rearrange(f3), ALU.subtract).then_inc(x2_done.sem, 1)
            if p1 is not None and s == 6:
                pool.wait_ge(hr_done.sem, hr_done.upto(p1, T))
                for t in range(T):
                    nc.gpsimd.tensor_tensor(hy[:, t, :], hr[:, t, :], y[:, t, :], ALU.add).then_inc(hy_done.sem, 1)
            if pn is not None and s == 6:
                pool.wait_ge(stat_done.sem, stat_done.upto(pn, 1))
                settle(pool)
                chain_p0.link(pool, nc.gpsimd.tensor_scalar(veps[:, :], mv[:, :, 1], EPS, None, ALU.add), pn)
                nc.gpsimd.tensor_tensor(rstd[:, :], veps[:, :], half[:, 0:T], ALU.pow).then_inc(rstd_done.sem, 1)
            if p1 is not None and s in (FIRST + 4, FIRST + 7):
                sum_parts((s - FIRST - 4) // 3, p1)

    shift_c = sb("shift_c", [P, 1])
    block = nc.Block()
    with block:
        @block.sync
        def _(sp):
            sp.dma_start(x_sb[:, :, :], x_v[0, :, :, :]).then_inc(x_in.sem, 16)
            sp.dma_start(adj_u[:, :, :], adj_v[0, :, :, :]).then_inc(adj_in.sem, 16)
            for n, w in enumerate(w_dram):
                if n:
                    sp.wait_ge(w_hi_done.sem, n)
                    sp.wait_ge(w_lo_done.sem, n)
                sp.dma_start(stage, w.rearrange("(c p) n -> p c n", p=P)).then_inc(w_in.sem, 16)
            for row, dst in ((bv, bv_b), (bf, bf_b), (Hb, Hb_b), (w_src, wsrc_b), (w_dst, wdst_b), (gb, gb_b)):
                sp.dma_start(dst[:, :], row.partition_broadcast(P).rearrange("p a n -> p (a n)")).then_inc(rows_in.sem, 16)
            for col, dst in ((bq, bq_c), (bk, bk_c)):
                sp.dma_start(dst[:, :], col).then_inc(rows_in.sem, 16)
            sync_body(sp, 1, 0, None, None)
            sync_body(sp, 2, 1, 0, None)
            sync_body(sp, 3, 2, 1, 0)
            with sp.Fori(3, PAIRS - 1) as i:
                sync_body(sp, i + 1, i, i - 1, i - 2)
            sync_body(sp, None, PAIRS - 1, PAIRS - 2, PAIRS - 3)
            sync_body(sp, None, None, PAIRS - 1, PAIRS - 2)
            sync_body(sp, None, None, None, PAIRS - 1)
            sp.wait_ge(stored.sem, 16 * T * PAIRS)

        @block.tensor
        def _(pe):
            pe.wait_ge(consts.sem, 5)
            pe.wait_ge(w_lo_done.sem, len(w_names))
            tensor_body(pe, 0, None, None)
            tensor_body(pe, 1, 0, None)
            tensor_body(pe, 2, 1, 0)
            with pe.Fori(3, PAIRS) as i:
                tensor_body(pe, i, i - 1, i - 2)
            tensor_body(pe, None, PAIRS - 1, PAIRS - 2)
            tensor_body(pe, None, None, PAIRS - 1)

        @block.vector
        def _(dve):
            nc.vector.memset(qz[:, :, :], 0.0).then_inc(consts.sem, 1)
            nc.vector.memset(shift_c[:, :], SHIFT).then_inc(consts.sem, 1)
            dve.wait_ge(consts.sem, 2)
            for n, name in enumerate(w_names):
                dve.wait_ge(w_hi_done.sem, n + 1)
                nc.vector.tensor_tensor(w_lo[name][:, :, :], stage, w_hi[name][:, :, :].bitcast(F32),
                                        ALU.subtract).then_inc(w_lo_done.sem, 1)
            dve.wait_ge(rows_in.sem, 16 * 8)
            vector_body(dve, 0, None, None, None)
            vector_body(dve, 1, 0, None, None)
            vector_body(dve, 2, 1, 0, None)
            vector_body(dve, 3, 2, 1, 0)
            with dve.Fori(3, PAIRS - 1) as i:
                vector_body(dve, i + 1, i, i - 1, i - 2)
            vector_body(dve, None, PAIRS - 1, PAIRS - 2, PAIRS - 3)
            vector_body(dve, None, None, PAIRS - 1, PAIRS - 2)
            vector_body(dve, None, None, None, PAIRS - 1)

        @block.scalar
        def _(act):
            for n, name in enumerate(w_names):
                act.wait_ge(w_in.sem, 16 * (n + 1))
                nc.scalar.activation(w_hi[name][:, :, :], stage, ACT.Copy).then_inc(w_hi_done.sem, 1)
            act.wait_ge(rows_in.sem, 16 * 8)
            act.wait_ge(consts.sem, 5)
            scalar_body(act, 0, None, None)
            scalar_body(act, 1, 0, None)
            scalar_body(act, 2, 1, 0)
            with act.Fori(3, PAIRS) as i:
                scalar_body(act, i, i - 1, i - 2)
            scalar_body(act, None, PAIRS - 1, PAIRS - 2)
            scalar_body(act, None, None, PAIRS - 1)

        @block.gpsimd
        def _(pool):
            set_up = nc.alloc_semaphore("set_up")
            nc.gpsimd.memset(half[:, :], -0.5).then_inc(set_up, 1)
            nc.gpsimd.memset(ident[:, :], 0.0).then_inc(set_up, 1)
            nc.gpsimd.memset(sel[:, :, :], 0.0).then_inc(set_up, 1)
            nc.gpsimd.memset(sT[:, :], 0.0).then_inc(set_up, 1)
            pool.wait_ge(set_up, 4)
            nc.gpsimd.affine_select(out=ident[:, :], in_=ident[:, :], compare_op=ALU.not_equal, fill=1.0, base=0,
                                    pattern=[[-1, P]], channel_multiplier=1).then_inc(set_up, 1)
            pool.wait_ge(set_up, 5)
            nc.gpsimd.tensor_copy(ident_b[:, :], ident[:, :]).then_inc(set_up, 1)
            for j in range(3):
                nc.gpsimd.affine_select(out=sel[:, :, :], in_=sel[:, :, :], compare_op=ALU.not_equal, fill=1.0,
                                        base=-AH * j, pattern=[[-1, AH], [0, P]], channel_multiplier=1).then_inc(set_up, 1)
                pool.wait_ge(set_up, 7 + j)
            pool.wait_ge(rows_in.sem, 16 * 8)
            pool.nop().then_inc(consts.sem, 1)
            pool.nop().then_inc(consts.sem, 2)
            gpsimd_body(pool, 0, None, None, None)
            gpsimd_body(pool, 1, 0, None, None)
            gpsimd_body(pool, 2, 1, 0, None)
            gpsimd_body(pool, 3, 2, 1, 0)
            with pool.Fori(3, PAIRS - 1) as i:
                gpsimd_body(pool, i + 1, i, i - 1, i - 2)
            gpsimd_body(pool, None, PAIRS - 1, PAIRS - 2, PAIRS - 3)
            gpsimd_body(pool, None, None, PAIRS - 1, PAIRS - 2)
            gpsimd_body(pool, None, None, None, PAIRS - 1)


_INS = ["x", "adj", "adjT", "Wq", "Wk", "Wv", "Wf", "W1", "HwT", "bq", "bk", "bv", "bf", "gb", "w_src", "w_dst", "Hb"]


def kernel(**inputs):
    import numpy as np
    import concourse.bacc as bacc
    from concourse.bass_utils import run_bass_kernel_spmd

    a = {k: np.asarray(v) for k, v in inputs.items()}
    adj = a["adj"]
    laid = {
        "x": a["x"], "adj": adj, "adjT": adj.transpose(0, 2, 1),
        "Wq": a["L0_gnn_Wq"], "Wk": a["L0_gnn_Wk"], "Wv": a["L0_gnn_Wv"], "Wf": a["L0_gnn_Wf"],
        "W1": a["L1_gnn_W"].transpose(1, 0, 2).reshape(H, H), "HwT": a["L1_gnn_H_w"].T,
        "bq": a["L0_gnn_bq"].reshape(KC, P).T, "bk": a["L0_gnn_bk"].reshape(KC, P).T, "bv": a["L0_gnn_bv"][None], "bf": a["L0_gnn_bf"][None],
        "gb": a["L1_gnn_b"][None], "w_src": a["L1_gnn_w_src"].reshape(1, H), "w_dst": a["L1_gnn_w_dst"].reshape(1, H),
        "Hb": a["L1_gnn_H_b"][None],
    }
    nc = bacc.Bacc("TRN2", target_bir_lowering=False, num_devices=1)
    arrays, args = {}, []
    for name in _INS:
        v = np.ascontiguousarray(laid[name])
        arrays[f"in_{name}"] = v
        args.append(nc.dram_tensor(f"in_{name}", v.shape, mybir.dt.from_np(v.dtype), kind="ExternalInput").ap())
    args.append(nc.dram_tensor("out", (GRAPHS, NODES, H), F32, kind="ExternalOutput").ap())
    graph_layers(nc, *args)
    r = run_bass_kernel_spmd(nc, [arrays], core_ids=[0])
    return r.results[0]["out"]
```

```python
import concourse.bass as bass
from concourse import mybir

F32 = mybir.dt.float32
F32R = mybir.dt.float32r
BF16 = mybir.dt.bfloat16
U8 = mybir.dt.uint8
ALU = mybir.AluOpType
ACT = mybir.ActivationFunctionType
AX = mybir.AxisListType

P = 128
GRAPHS, NODES, H = 32, 256, 384
PAIRS = GRAPHS // 2
T = 2 * NODES // P
W = T * P
KC = H // P
NH, HD = 6, 64
AH, OD = 12, 32
E1 = OD + 1
UNITS = 2 * NH
SLOTS = 10
PROJECTIONS = [("Q", c) for c in range(KC)] + [("K", c) for c in range(KC)] + [("V", t) for t in range(T)]
STEPS = UNITS + 3
FIRST = 9
EARLY = 6
GATE = 3
CONTEXT = (7, 11)
LATER = (4, 8)
FACTORS = (6, 7, 9, 11)
EPS = 1e-5
MASKED = -9000000000000000.0
LEAK = 0.2
SHIFT = 40.0

def unit(n):
    c, g, side = n // 4, (n // 2) % 2, n % 2
    return c, g, side, 2 * c + side


class Signal:

    def __init__(self, nc, name, per):
        self.sem, self.per = nc.alloc_semaphore(name), per

    def upto(self, p, k):
        return p * self.per + k


def due(p, k):
    return not isinstance(p, int) or p > 0 or (p == 0 and k > 0)


class Chain:

    def __init__(self, nc, name):
        self.sem, self.per, self.count = nc.alloc_semaphore(name), None, 0

    def start(self, p):
        if self.per is None and self.count:
            self.per = self.count
        assert isinstance(p, int) and p == 0 or self.per is not None
        self.count = 0

    def link(self, eng, ins, p):
        self.count += 1
        ins.then_inc(self.sem, 1)
        eng.wait_ge(self.sem, (0 if isinstance(p, int) and p == 0 else p * self.per) + self.count)


def _banks():
    layer0 = [("A", c) for c in range(KC)] + PROJECTIONS + [("E", c) for c in range(KC)]
    for s in range(UNITS + 2):
        layer0 += [("S", s)] * (s < UNITS) + [("PT", s - 2)] * (s >= 2)
    layer0 += [("D", t) for t in range(T)]
    layer0 = [(x, n % 3) for n, x in enumerate(layer0)]
    layer1 = []
    for s in range(GATE + T):
        layer1 += [("h", s)] * (s < T) + [("gate", s - GATE)] * (s >= GATE)
    layer1 += [("sT", 0)]
    layer1 = [(x, 4 + n % 4) for n, x in enumerate(layer1)]
    layer1 += [(("SR", n), 4 + (n + 1) % 2) for n in range(UNITS)]
    uses, totals = {}, []
    for lot in (layer0, layer1):
        last, count = {}, 0
        for x, b in lot:
            uses[x] = (b, count, last.get(b, ()))
            last[b] = (x, *last.get(b, ()))
            count += x[0] != "E"
        for x, (b, n, earlier) in list(uses.items()):
            if not earlier:
                uses[x] = (b, n, (last.get(b, ((None, 0),))[0], "pair before"))
        totals.append(count)
    return uses, totals[0], totals[1]


USES, USES0, USES1 = _banks()


def graph_layers(nc, x, adj, adjT, Wq, Wk, Wv, Wf, W1, HwT, bq, bk, bv, bf, gb, w_src, w_dst, Hb, out):
    x_v = x.rearrange("(a g) (c q) f -> a q (g c) f", g=2, q=P)
    adj_v = adj.rearrange("(a g) (c q) k -> a q (g c) k", g=2, q=P)
    adjT_v = adjT.rearrange("(a g) (c q) k -> a q (g c) k", g=2, q=P)
    out_v = out.rearrange("(a g) (c q) f -> a q (g c) f", g=2, q=P)

    def sb(name, shape, dt=F32):
        return nc.alloc_sbuf_tensor(name, shape, dt)

    w_names = ("Wq", "Wk", "Wv", "Wf", "W1", "Hw")
    w_dram = (Wq, Wk, Wv, Wf, W1, HwT)
    w_hi = {n: sb(n + "_hi", [P, KC, H], F32R) for n in w_names}
    w_lo = {n: sb(n + "_lo", [P, KC, H], F32R) for n in w_names}
    bf_b, Hb_b = sb("bf_b", [P, H]), sb("Hb_b", [P, H])
    wsrc_b, wdst_b, gb_b = sb("wsrc_b", [P, H]), sb("wdst_b", [P, H]), sb("gb_b", [P, OD])
    bq_c, bq8_c, bk_c, bv_c = sb("bq_c", [P, KC]), sb("bq8_c", [P, KC]), sb("bk_c", [P, KC]), sb("bv_c", [P, KC])
    ident = sb("ident", [P, P])
    ident_b = sb("ident_b", [P, P], BF16)
    sel = sb("sel", [P, AH, P], BF16)
    half = sb("half", [P, 2 * T])
    x_sb, xb = sb("x_sb", [P, T, H]), sb("xb", [P, T, H])
    adj_u = sb("adj_u", [P, T, NODES], U8)
    mask = sb("mask", [P, T, NODES], BF16)
    stats, mv, rstd, veps = sb("stats", [P, T, 6]), sb("mv", [P, T, 2]), sb("rstd", [P, T]), sb("veps", [P, T])
    hn = sb("hn", [P, T, H])
    hT_hi, hT_lo = sb("hT_hi", [P, KC, W], F32R), sb("hT_lo", [P, KC, W], F32R)
    qT, kT, v_sb = sb("qT", [P, KC, W]), sb("kT", [P, KC, W]), sb("v_sb", [P, T, H])
    probs = sb("probs", [P, 4, 2, NODES])
    probsT = sb("probsT", [P, 3, 2, NODES])
    nmax, rsum, rinv = sb("nmax", [P, 4, 2]), sb("rsum", [P, 4, 2]), sb("rinv", [P, 4, 2])
    y = sb("y", [P, T, H])
    adjT_u = sb("adjT_u", [P, T, NODES], U8)
    adj_p, adj_n = sb("adj_p", [P, T, NODES], BF16), sb("adj_n", [P, T, NODES], BF16)
    stats2, mv2, rstd2, veps2 = sb("stats2", [P, T, 6]), sb("mv2", [P, T, 2]), sb("rstd2", [P, T]), sb("veps2", [P, T])
    negmean2, shift2 = sb("negmean2", [P, T]), sb("shift2", [P, T])
    hr, hy = sb("hr", [P, T, H]), sb("hy", [P, T, H])
    h1 = sb("h1", [P, T, AH, OD])
    gl = sb("gl", [P, T, H])
    sd = sb("sd", [P, T, 2 * AH])
    dmax2, dmax = sb("dmax2", [P, 2 * AH]), sb("dmax", [P, 2 * AH])
    s_rest = sb("s_rest", [P, T, AH])
    s_parts = sb("s_parts", [P, T, 3 * AH], BF16)
    sT = sb("sT", [P, W], BF16)
    d_neg = sb("d_neg", [P, T, AH])
    u_sb, m_sb = sb("u_sb", [P, T, AH]), sb("m_sb", [P, T, AH])
    e_in, e_out = sb("e_in", [P, T, 3, AH]), sb("e_out", [P, T, 3, AH])
    e_leak = sb("e_leak", [P, T, AH])
    a_neg = sb("a_neg", [P, T, AH])
    G = sb("G", [P, 2, 2, AH, E1])
    g_flat = G[:, :, :, :, :].rearrange("p s r h e -> p (s r h e)")
    tw = g_flat[:, 0:4 * H].rearrange("p (s h e) -> p s h e", s=2, e=OD)
    stage = [y[:, 0:KC, :], hr[:, 0:KC, :], hy[:, 0:KC, :], gl[:, 0:KC, :], h1[:, 0:KC, :, :].rearrange("p c h e -> p c (h e)"),
             g_flat[:, 0:KC * H].rearrange("p (c n) -> p c n", c=KC)]
    X = sb("X", [P, T, 3, 2, AH, E1], BF16)
    Mp = sb("Mp", [P, 2, 2, 2, NODES], BF16)
    part1, part2 = sb("part1", [P, 2, NH, E1]), sb("part2", [P, 2, NH, E1])
    dinv = sb("dinv", [P, 2, NH])
    e_sb = sb("e_sb", [P, 2, H])
    th = e_sb[:, :, :].rearrange("p s (h e) -> p s h e", e=OD)
    cT_hi, cT_lo = hT_hi, hT_lo

    bank = [nc.alloc_psum_tensor(f"bank{b}", [P, 512], F32) for b in range(8)]
    ctx = bank[3]
    acc = [bank[6], bank[7]]

    def sig(name, per):
        return Signal(nc, name, per)

    w_in = [sig("w_in_" + n, 0) for n in w_names]
    w_hi_done, w_lo_done = sig("w_hi_done", 0), sig("w_lo_done", 0)
    rows_in, consts = sig("rows_in", 0), sig("consts", 0)
    x_in, adj_in, adjT_in = sig("x_in", 16), sig("adj_in", 16), sig("adjT_in", 16)
    use0, use1 = sig("use0", USES0), sig("use1", USES1)
    stat_done, rstd_done, ln1_done = sig("stat_done", 1), sig("rstd_done", 1), sig("ln1_done", T)
    xb_done, mask_done = sig("xb_done", 1), sig("mask_done", 1)
    hi_done, lo_done = sig("hi_done", KC), sig("lo_done", KC)
    e_filled = sig("e_filled", KC)
    q_done, k_done, v_done = sig("q_done", KC), sig("k_done", KC), sig("v_done", T)
    max_done, exp_done, rinv_done = sig("max_done", UNITS), sig("exp_done", 2 * UNITS), sig("rinv_done", UNITS)
    pn0_done, pn1_done = sig("pn0_done", UNITS), sig("pn1_done", UNITS)
    pt_done, pv_done = sig("pt_done", UNITS), sig("pv_done", UNITS)
    chi_done, clo_done, y_done = sig("chi_done", KC), sig("clo_done", KC), sig("y_done", T)
    adjT_done, adjN_done = sig("adjT_done", 1), sig("adjN_done", 1)
    stat2_done, rstd2_done, ln2_done = sig("stat2_done", 1), sig("rstd2_done", 1), sig("ln2_done", T)
    hr_done, hy_done = sig("hr_done", T), sig("hy_done", T)
    hi2_done, lo2_done = sig("hi2_done", KC), sig("lo2_done", KC)
    th_done, h1_done, gl_done, gate_done = sig("th_done", T), sig("h1_done", T), sig("gl_done", T), sig("gate_done", T)
    tw_done, sd_done, dm_done, dmax_done = sig("tw_done", T), sig("sd_done", T), sig("dm_done", 1), sig("dmax_done", 1)
    parts_done, sT_done = sig("parts_done", 1), sig("sT_done", 1)
    ein_done, e_done, dneg_done, aneg_done = sig("ein_done", 1), sig("e_done", 2), sig("dneg_done", 1), sig("aneg_done", 1)
    g1_done, g2_done = sig("g1_done", T), sig("g2_done", T)
    x0_done, r_done, x1_done, x2_done = sig("x0_done", T), sig("r_done", T), sig("x1_done", T), sig("x2_done", T)
    m_done, mm_done = sig("m_done", UNITS), sig("mm_done", UNITS)
    acc_out, num_done, f_done, v1_done = sig("acc_out", 2 * T), sig("num_done", 2 * T), sig("f_done", 2 * T), sig("v1_done", T)
    e1_done, elu_done, w1_done, out_done, stored = (sig("e1_done", T), sig("elu_done", T), sig("w1_done", T),
                                                   sig("out_done", T), [sig("stored01", 16), sig("stored23", 16)])
    chain_d0, chain_d1 = Chain(nc, "chain_d0"), Chain(nc, "chain_d1")
    chain_p0, chain_p1 = Chain(nc, "chain_p0"), Chain(nc, "chain_p1")
    chain_a2, chain_d2 = Chain(nc, "chain_a2"), Chain(nc, "chain_d2")

    def bank_of(name, k):
        return bank[USES[name, k][0]]

    def filled(name, k):
        return USES[name, k][1] + 1

    def read(name, k):
        return {
            "A": (lo_done, k + 1), "Q": (q_done, k + 1), "K": (k_done, k + 1), "V": (v_done, k + 1),
            "S": (exp_done, 2 * k + 2), "PT": (pt_done, k + 1), "D": (y_done, k + 1),
            "E": (lo2_done, k + 1), "h": (h1_done, k + 1), "gate": (gl_done, k + 1), "sT": (sT_done, 1),
            "SR": (m_done, k + 1), "acc": (acc_out, 2 * T),
        }[name]

    def before(p, name, k):
        b, _, earlier = USES[name, k]
        if earlier[1:] == ("pair before",):
            what = ("acc", 0) if b in (6, 7) else earlier[0]
            return (*read(*what), p - 1)
        if earlier[0][0] == "E":
            return (*read(*earlier[1]), p) if isinstance(p, int) and p == 0 else (*read(*earlier[0]), p - 1)
        return (*read(*earlier[0]), p)

    def used_before(p, name, k):
        signal, count, pair = before(p, name, k)
        return due(pair, count)

    def reader_done(p, name, k):
        signal, count, pair = before(p, name, k)
        return signal.sem, signal.upto(pair, count)

    def seg(n):
        return slice(n * P, (n + 1) * P)

    def gat(n):
        return n // 6, 2 * (n % 6)

    waited = nc.alloc_semaphore("waited")

    def settle(eng):
        eng.sem_inc(waited, 1)

    def sync_body(sp, pn, p0, p1, p2):
        if pn is not None:
            if due(pn - 1, 1):
                sp.wait_ge(ln1_done.sem, ln1_done.upto(pn - 1, T))
                settle(sp)
                sp.wait_ge(xb_done.sem, xb_done.upto(pn - 1, 1))
                settle(sp)
            sp.dma_start(x_sb[:, :, :], x_v[pn, :, :, :]).then_inc(x_in.sem, 16)
            if due(pn - 1, 1):
                sp.wait_ge(mask_done.sem, mask_done.upto(pn - 1, 1))
                settle(sp)
            sp.dma_start(adj_u[:, :, :], adj_v[pn, :, :, :]).then_inc(adj_in.sem, 16)
        if p2 is not None:
            for g in range(2):
                sp.wait_ge(out_done.sem, out_done.upto(p2, 2 * g + 2))
                settle(sp)
                sp.dma_start(out_v[p2, :, 2 * g:2 * g + 2, :],
                             hy[:, 2 * g:2 * g + 2, :]).then_inc(stored[g].sem, 16)
        if p0 is not None:
            if due(p0 - 1, 2):
                sp.wait_ge(adjT_done.sem, adjT_done.upto(p0 - 1, 1))
                settle(sp)
                sp.wait_ge(adjN_done.sem, adjN_done.upto(p0 - 1, 1))
                settle(sp)
            sp.dma_start(adjT_u[:, :, :], adjT_v[p0, :, :, :]).then_inc(adjT_in.sem, 16)

    def chunk_product(o, c, stat_hi, stat_lo, mov_hi, mov_lo):
        nc.tensor.matmul(o, stat_hi, mov_hi, start=c == 0, stop=False, skip_group_check=True)
        nc.tensor.matmul(o, stat_hi, mov_lo, start=False, stop=False, skip_group_check=True)
        return nc.tensor.matmul(o, stat_lo, mov_hi, start=False, stop=c == KC - 1, skip_group_check=True)

    def project_T(o, name, k, c):
        return chunk_product(o[:, :], c, w_hi[name][:, c, seg(k)], w_lo[name][:, c, seg(k)], hT_hi[:, c, :], hT_lo[:, c, :])

    def project(o, name, t, c):
        return chunk_product(o[:, 0:H], c, hT_hi[:, c, seg(t)], hT_lo[:, c, seg(t)], w_hi[name][:, c, :], w_lo[name][:, c, :])

    def tensor_body(pe, p0, p1, p2):
        def s_rows(n, p):
            g, head = gat(n)
            if used_before(p, "SR", n):
                pe.wait_ge(*reader_done(p, "SR", n))
            o = bank_of("SR", n)
            for k in range(2):
                last = nc.tensor.matmul(o[:, k * NODES:(k + 1) * NODES], sel[:, head + k, :],
                                        sT[:, g * NODES:(g + 1) * NODES], start=True, stop=True)
            last.then_inc(use1.sem, 1)

        def gather(n, p):
            g, head = gat(n)
            first = head - head % NH
            if n == 0:
                pe.wait_ge(adjT_done.sem, adjT_done.upto(p, 1))
                pe.wait_ge(gl_done.sem, gl_done.upto(p, T))
                pe.wait_ge(h1_done.sem, h1_done.upto(p, T))
            elif n % 3 == 0:
                pe.wait_ge(acc_out.sem, acc_out.upto(p, 2 * (n // 3)))
            if n % 6 == 0:
                pe.wait_ge(x2_done.sem, x2_done.upto(p, 2 * g + 2))
            if n % 3 == 0:
                for i in range(2):
                    for j in range(2):
                        for part in range(3):
                            nc.tensor.matmul(acc[i][:, NH * E1:2 * NH * E1], adj_p[:, 2 * g + j, seg(i)],
                                             X[:, 2 * g + j, part, 1, first:first + NH, :],
                                             start=j == 0 and part == 0, stop=False, skip_group_check=True)
            pe.wait_ge(m_done.sem, m_done.upto(p, n + 1))
            for k in range(2):
                col = (head + k) % NH
                for i in range(2):
                    o = acc[i][:, 0:2 * NH * E1].rearrange("p (r h e) -> p r h e", r=2, h=NH)[:, :, col, :]
                    for j in range(2):
                        for part in range(3):
                            last = nc.tensor.matmul(o, Mp[:, n % 2, k, j, seg(i)], X[:, 2 * g + j, part, :, head + k, :],
                                                    start=False, stop=False, skip_group_check=True)
            last.then_inc(mm_done.sem, 1)

        def scores(n):
            c, g, side, head = unit(n)
            rows = slice(side * HD, (side + 1) * HD)
            if used_before(p0, "S", n):
                pe.wait_ge(*reader_done(p0, "S", n))
            o = bank_of("S", n)
            if n == 0:
                pe.wait_ge(q_done.sem, q_done.upto(p0, KC))
                pe.wait_ge(k_done.sem, k_done.upto(p0, KC))
                pe.wait_ge(mask_done.sem, mask_done.upto(p0, 1))
            for q in range(2):
                t = 2 * g + q
                o_q = o[:, q * NODES:(q + 1) * NODES]
                nc.tensor.matmul(o_q, qT[rows, c, seg(t)], kT[rows, c, g * NODES:(g + 1) * NODES], start=True, stop=False)
                last = nc.tensor.matmul(o_q, ident_b[:, :], mask[:, t, :], start=False, stop=True)
            last.then_inc(use0.sem, 1)

        def probs_T(n):
            if used_before(p0, "PT", n):
                pe.wait_ge(*reader_done(p0, "PT", n))
            o = bank_of("PT", n)
            for q in range(2):
                pn = (pn0_done, pn1_done)[q]
                pe.wait_ge(pn.sem, pn.upto(p0, n + 1))
                for k in range(2):
                    last = nc.tensor.transpose(o[:, k * NODES + q * P:k * NODES + (q + 1) * P],
                                               probs[:, n % 4, q, seg(k)], ident[:, :])
            last.then_inc(use0.sem, 1)

        def context(n):
            c, g, side, head = unit(n)
            pe.wait_ge(pt_done.sem, pt_done.upto(p0, n + 1))
            if n == 0:
                pe.wait_ge(v_done.sem, v_done.upto(p0, T))
            if n == 0 and due(p0 - 1, KC):
                pe.wait_ge(clo_done.sem, clo_done.upto(p0 - 1, KC))
            if n % 4 == 0 and c > 0:
                pe.wait_ge(clo_done.sem, clo_done.upto(p0, c))
            for k in range(2):
                last = nc.tensor.matmul(ctx[side * HD:(side + 1) * HD, g * NODES:(g + 1) * NODES],
                                        v_sb[:, 2 * g + k, head * HD:(head + 1) * HD], probsT[:, n % 3, k, :],
                                        start=k == 0, stop=k == 1)
            last.then_inc(pv_done.sem, 1)

        if p2 is not None:
            s_rows(EARLY + 1, p2)
        if p0 is not None:
            for c in range(KC):
                if used_before(p0, "A", c):
                    pe.wait_ge(*reader_done(p0, "A", c))
                o = bank_of("A", c)
                for t in range(T):
                    if c == 0:
                        pe.wait_ge(ln1_done.sem, ln1_done.upto(p0, t + 1))
                    last = nc.tensor.transpose(o[:, seg(t)], hn[:, t, seg(c)], ident[:, :])
                last.then_inc(use0.sem, 1)
        if p2 is not None:
            gather(EARLY, p2)
        for slot in range(SLOTS):
            n = EARLY + 1 + slot
            if p2 is not None and n + 1 < UNITS:
                s_rows(n + 1, p2)
            if p0 is not None:
                what, k = PROJECTIONS[slot]
                if isinstance(p0, int) and p0 == 0:
                    pe.wait_ge(w_lo_done.sem, w_names.index("W" + what.lower()) + 1)
                if used_before(p0, what, k):
                    pe.wait_ge(*reader_done(p0, what, k))
                o = bank_of(what, k)
                for c in range(KC):
                    if slot == 0:
                        pe.wait_ge(hi_done.sem, hi_done.upto(p0, c + 1))
                        pe.wait_ge(lo_done.sem, lo_done.upto(p0, c + 1))
                    if what == "V":
                        last = project(o, "Wv", k, c)
                    else:
                        last = project_T(o, {"Q": "Wq", "K": "Wk"}[what], k, c)
                last.then_inc(use0.sem, 1)
            if p2 is not None and n < UNITS:
                gather(n, p2)
        if p1 is not None:
            for c in range(KC):
                if p0 is not None:
                    pe.wait_ge(*reader_done(p0, "E", c))
                o = bank_of("E", c)
                for t in range(T):
                    if c == 0:
                        pe.wait_ge(ln2_done.sem, ln2_done.upto(p1, t + 1))
                    last = nc.tensor.transpose(o[:, seg(t)], hn[:, t, seg(c)], ident[:, :])
                last.then_inc(e_filled.sem, 1)
        for s in range(STEPS):
            if p0 is not None and s < UNITS:
                scores(s)
            for what, name, t in (("h", "W1", s), ("gate", "Hw", s - GATE)):
                if p1 is not None and 0 <= t < T:
                    if used_before(p1, what, t):
                        pe.wait_ge(*reader_done(p1, what, t))
                    for c in range(KC):
                        if s == 0:
                            pe.wait_ge(hi2_done.sem, hi2_done.upto(p1, c + 1))
                            pe.wait_ge(lo2_done.sem, lo2_done.upto(p1, c + 1))
                        last = project(bank_of(what, t), name, t, c)
                    last.then_inc(use1.sem, 1)
            if p0 is not None and 0 <= s - 2 < UNITS:
                probs_T(s - 2)
            if p1 is not None and s == FIRST - 2:
                if used_before(p1, "sT", 0):
                    pe.wait_ge(*reader_done(p1, "sT", 0))
                pe.wait_ge(parts_done.sem, parts_done.upto(p1, 1))
                settle(pe)
                o_b = bank_of("sT", 0)[:, :].bitcast(BF16)
                for t in range(T):
                    last = nc.tensor.transpose(o_b[0:3 * AH, seg(t)], s_parts[:, t, :], ident_b[:, :])
                last.then_inc(use1.sem, 1)
            if p1 is not None and s == FIRST:
                pe.wait_ge(sT_done.sem, sT_done.upto(p1, 1))
            if p1 is not None and 0 <= s - FIRST < EARLY:
                s_rows(s - FIRST, p1)
            if p0 is not None and 0 <= s - 3 < UNITS and s - 3 not in LATER:
                if s - 4 in LATER:
                    context(s - 4)
                context(s - 3)
            if p1 is not None and 0 <= s - FIRST - 1 < EARLY - 1:
                gather(s - FIRST - 1, p1)
        def output(t, chunks):
            for c in chunks:
                last = project(bank_of("D", t), "Wf", t, c)
            return last

        if p1 is not None:
            s_rows(EARLY, p1)
        if p0 is not None:
            if isinstance(p0, int) and p0 == 0:
                pe.wait_ge(w_lo_done.sem, len(w_names))
            pe.wait_ge(chi_done.sem, chi_done.upto(p0, KC - 1))
            pe.wait_ge(clo_done.sem, clo_done.upto(p0, KC - 1))
            for t in range(3):
                if used_before(p0, "D", t):
                    pe.wait_ge(*reader_done(p0, "D", t))
                output(t, range(KC - 1))
        if p1 is not None:
            gather(EARLY - 1, p1)
        if p0 is not None:
            pe.wait_ge(chi_done.sem, chi_done.upto(p0, KC))
            pe.wait_ge(clo_done.sem, clo_done.upto(p0, KC))
            for t in range(3):
                output(t, [KC - 1]).then_inc(use0.sem, 1)
            for t in range(3, T):
                pe.wait_ge(*reader_done(p0, "D", t))
                output(t, range(KC)).then_inc(use0.sem, 1)

    def vector_body(dve, pn, p0, p1, p2):
        by_graph = "p (g c) h -> p g c h"
        s_of = sd[:, :, 0:AH]
        d_of = sd[:, :, AH:2 * AH]
        d4 = d_of.rearrange(by_graph, c=2)
        D4 = dmax[:, :].rearrange("p (g h) -> p g h", g=2).unsqueeze(2).broadcast_to([P, 2, 2, AH])
        if pn is not None:
            chain_d0.start(pn)
        if p1 is not None:
            chain_d1.start(p1)
        if p2 is not None:
            chain_d2.start(p2)

        def neighbours(n, p):
            g, head = gat(n)
            dve.wait_ge(use1.sem, use1.upto(p, filled("SR", n)))
            if n >= 2:
                dve.wait_ge(mm_done.sem, mm_done.upto(p, n - 1))
            elif due(p - 1, UNITS):
                dve.wait_ge(mm_done.sem, mm_done.upto(p - 1, UNITS))
            o = bank_of("SR", n)
            for k in range(2):
                for j in range(2):
                    t = 2 * g + j
                    last = nc.vector.scalar_tensor_tensor(
                        Mp[:, n % 2, k, j, :], o[:, k * NODES:(k + 1) * NODES], d_neg[:, t, head + k:head + k + 1],
                        adj_n[:, t, :], ALU.is_ge, ALU.mult)
            last.then_inc(m_done.sem, 1)

        def acc_leave(q, p):
            g, hf = q // 2, q % 2
            heads = slice(hf * NH, (hf + 1) * NH)
            dve.wait_ge(mm_done.sem, mm_done.upto(p, 3 * q + 3))
            if q > 0:
                dve.wait_ge(f_done.sem, f_done.upto(p, 2 * q))
            elif due(p - 1, 2 * T):
                dve.wait_ge(f_done.sem, f_done.upto(p - 1, 2 * T))
            for i in range(2):
                t = 2 * g + i
                left, right = acc[i][:, 0:NH * E1], acc[i][:, NH * E1:2 * NH * E1]
                nc.vector.tensor_tensor(part1[:, i, :, :], left.rearrange("p (h e) -> p h e", h=NH),
                                        a_neg[:, t, heads].unsqueeze(2).broadcast_to([P, NH, E1]), ALU.mult)
                nc.vector.tensor_tensor(part2[:, i, :, :], right.rearrange("p (h e) -> p h e", h=NH),
                                        e_out[:, t, 1, heads].unsqueeze(2).broadcast_to([P, NH, E1]),
                                        ALU.mult).then_inc(acc_out.sem, 1)

        def divide(q, p, chain):
            g, hf = q // 2, q % 2
            heads = slice(hf * NH, (hf + 1) * NH)
            for i in range(2):
                dve.wait_ge(num_done.sem, num_done.upto(p, 2 * q + i + 1))
                last = nc.vector.reciprocal(dinv[:, i, :], part1[:, i, :, OD])
            chain.link(dve, last, p)
            for i in range(2):
                nc.vector.tensor_tensor(h1[:, 2 * g + i, heads, :], part1[:, i, :, 0:OD],
                                        dinv[:, i, :].unsqueeze(2).broadcast_to([P, NH, OD]),
                                        ALU.mult).then_inc(f_done.sem, 1)

        def elu(t):
            dve.wait_ge(e1_done.sem, e1_done.upto(p2, t + 1))
            v = h1[:, t, :, :].rearrange("p h e -> p (h e)")
            nc.vector.scalar_tensor_tensor(v, e_sb[:, t % 2, :], -1.0, v, ALU.add, ALU.max).then_inc(elu_done.sem, 1)

        def mix(tiles):
            for t in tiles:
                dve.wait_ge(w1_done.sem, w1_done.upto(p2, t + 1))
                dve.wait_ge(gate_done.sem, gate_done.upto(p2, t + 1))
                v = h1[:, t, :, :].rearrange("p h e -> p (h e)")
                last = nc.vector.scalar_tensor_tensor(v, gl[:, t, :], 1.0, v, ALU.add, ALU.mult)
            chain_d2.link(dve, last, p2)
            for t in tiles:
                v = h1[:, t, :, :].rearrange("p h e -> p (h e)")
                nc.vector.scalar_tensor_tensor(hy[:, t, :], v, 0.5, hy[:, t, :], ALU.mult, ALU.add).then_inc(out_done.sem, 1)

        def context_low(c):
            dve.wait_ge(pv_done.sem, pv_done.upto(p0, 4 * c + 4))
            dve.wait_ge(chi_done.sem, chi_done.upto(p0, c + 1))
            nc.vector.scalar_tensor_tensor(cT_lo[:, c, :], ctx[:, :], bv_c[:, c:c + 1], cT_hi[:, c, :].bitcast(F32),
                                           ALU.add, ALU.subtract).then_inc(clo_done.sem, 1)

        if p0 is not None:
            for c in range(KC):
                dve.wait_ge(use0.sem, use0.upto(p0, filled("A", c)))
                o = bank_of("A", c)
                dve.wait_ge(hi_done.sem, hi_done.upto(p0, c + 1))
                nc.vector.scalar_tensor_tensor(hT_lo[:, c, :], o[:, :], 0.0, hT_hi[:, c, :].bitcast(F32),
                                               ALU.max, ALU.subtract).then_inc(lo_done.sem, 1)
        if p2 is not None:
            neighbours(EARLY + 1, p2)
        for slot in range(SLOTS + 1):
            if p2 is not None and slot in (2, 5):
                acc_leave(slot // 3 + 2, p2)
            if p2 is not None and EARLY + 2 + slot < UNITS:
                neighbours(EARLY + 2 + slot, p2)
            if p1 is not None and slot == 3:
                dve.wait_ge(y_done.sem, y_done.upto(p1, T))
                for t in range(T):
                    last = nc.vector.bn_stats(stats2[:, t, :], y[:, t, :])
                chain_d1.link(dve, last, p1)
                settle(dve)
                for t in range(T):
                    last = nc.vector.bn_aggr(mv2[:, t, :], stats2[:, t, :])
                last.then_inc(stat2_done.sem, 1)
            if p2 is not None and slot in (0, 3, 6):
                divide(slot // 3 + 1, p2, chain_d2)
            if p2 is not None and slot in (4, 9):
                for t in ((0, 1) if slot == 4 else (2, 3)):
                    elu(t)
            if p2 is not None and slot == 7:
                mix((0, 1))
        if p1 is not None:
            for c in range(KC):
                dve.wait_ge(e_filled.sem, e_filled.upto(p1, c + 1))
                o = bank_of("E", c)
                dve.wait_ge(hi2_done.sem, hi2_done.upto(p1, c + 1))
                nc.vector.scalar_tensor_tensor(hT_lo[:, c, :], o[:, :], 0.0, hT_hi[:, c, :].bitcast(F32),
                                               ALU.max, ALU.subtract).then_inc(lo2_done.sem, 1)
        if p2 is not None:
            mix((2, 3))
        for s in range(STEPS):
            if p1 is not None and s == FIRST + 4:
                dve.wait_ge(aneg_done.sem, aneg_done.upto(p1, 1))
                acc_leave(0, p1)
            if p0 is not None and 0 <= s - 1 < UNITS:
                n = s - 1
                dve.wait_ge(exp_done.sem, exp_done.upto(p0, 2 * n + 2))
                nc.vector.reciprocal(rinv[:, n % 4, :], rsum[:, n % 4, :]).then_inc(rinv_done.sem, 1)
            if p0 is not None and s < UNITS:
                dve.wait_ge(use0.sem, use0.upto(p0, filled("S", s)))
                o = bank_of("S", s)
                nc.vector.tensor_reduce(nmax[:, s % 4, :], o[:, :].rearrange("p (q k) -> p q k", q=2),
                                        AX.X, ALU.max, negate=True).then_inc(max_done.sem, 1)
            if p0 is not None and s in CONTEXT:
                context_low(CONTEXT.index(s))
            if p0 is not None and 0 <= s - 1 < UNITS:
                n = s - 1
                dve.wait_ge(rinv_done.sem, rinv_done.upto(p0, n + 1))
                nc.vector.tensor_scalar(probs[:, n % 4, 1, :], probs[:, n % 4, 1, :], rinv[:, n % 4, 1:2], None,
                                        ALU.mult).then_inc(pn1_done.sem, 1)
            if p1 is not None and 0 <= s - GATE < T:
                t = s - GATE
                dve.wait_ge(use1.sem, use1.upto(p1, filled("gate", t)))
                o = bank_of("gate", t)
                nc.vector.tensor_tensor(gl[:, t, :], o[:, 0:H], Hb_b[:, :], ALU.add).then_inc(gl_done.sem, 1)
            if p1 is not None and 0 <= s - 1 < T:
                t = s - 1
                dve.wait_ge(tw_done.sem, tw_done.upto(p1, t + 1))
                nc.vector.tensor_reduce(sd[:, t, :], tw[:, t % 2, :, :], AX.X, ALU.add).then_inc(sd_done.sem, 1)
            if pn is not None and s == 0:
                dve.wait_ge(x_in.sem, x_in.upto(pn, 16))
                for t in range(T):
                    last = nc.vector.bn_stats(stats[:, t, :], x_sb[:, t, :])
                chain_d0.link(dve, last, pn)
                settle(dve)
                for t in range(T):
                    last = nc.vector.bn_aggr(mv[:, t, :], stats[:, t, :])
                last.then_inc(stat_done.sem, 1)
            if p1 is not None and s == 2:
                dve.wait_ge(adjT_in.sem, adjT_in.upto(p1, 16))
                nc.vector.tensor_scalar(adj_n[:, :, :], adjT_u[:, :, :], -1.0, None, ALU.mult).then_inc(adjN_done.sem, 1)
            if pn is not None and s == 3:
                dve.wait_ge(stat_done.sem, stat_done.upto(pn, 1))
                dve.wait_ge(rstd_done.sem, rstd_done.upto(pn, 1))
                if p1 is not None:
                    dve.wait_ge(hr_done.sem, hr_done.upto(p1, T))
                    dve.wait_ge(e_filled.sem, e_filled.upto(p1, KC))
                elif p0 is not None:
                    dve.wait_ge(use0.sem, use0.upto(p0, filled("A", KC - 1)))
                for t in range(T):
                    nc.vector.tensor_scalar(hn[:, t, :], x_sb[:, t, :], mv[:, t, 0:1], rstd[:, t:t + 1],
                                            ALU.subtract, ALU.mult).then_inc(ln1_done.sem, 1)
            if p1 is not None and s == 4:
                dve.wait_ge(sd_done.sem, sd_done.upto(p1, T))
                nc.vector.tensor_tensor(dmax2[:, :].rearrange("p (g h) -> p g h", g=2), d4[:, :, 0, :],
                                        d4[:, :, 1, :], ALU.max).then_inc(dm_done.sem, 1)
                sp3 = s_parts[:, :, :].rearrange("p t (j h) -> p t j h", j=3)
                chain_d1.link(dve, nc.vector.tensor_copy(sp3[:, :, 0, :], s_of), p1)
                chain_d1.link(dve, nc.vector.tensor_tensor(s_rest[:, :, :], s_of, sp3[:, :, 0, :], ALU.subtract), p1)
                chain_d1.link(dve, nc.vector.tensor_copy(sp3[:, :, 1, :], s_rest[:, :, :]), p1)
                nc.vector.tensor_tensor(sp3[:, :, 2, :], s_rest[:, :, :], sp3[:, :, 1, :], ALU.subtract).then_inc(parts_done.sem, 1)
                nc.vector.tensor_scalar(d_neg[:, :, :], d_of, -1.0, None, ALU.mult).then_inc(dneg_done.sem, 1)
            if p1 is not None and s == 5:
                dve.wait_ge(dmax_done.sem, dmax_done.upto(p1, 1))
                chain_d1.link(dve, nc.vector.tensor_tensor(u_sb[:, :, :].rearrange(by_graph, c=2),
                                                           s_of.rearrange(by_graph, c=2), D4, ALU.add), p1)
                chain_d1.link(dve, nc.vector.scalar_tensor_tensor(m_sb[:, :, :], u_sb[:, :, :], LEAK, u_sb[:, :, :],
                                                                  ALU.mult, ALU.max), p1)
                nc.vector.tensor_tensor(e_in[:, :, 0, :], u_sb[:, :, :], m_sb[:, :, :], ALU.subtract)
                nc.vector.scalar_tensor_tensor(e_in[:, :, 1, :], u_sb[:, :, :], LEAK, m_sb[:, :, :], ALU.mult, ALU.subtract)
                nc.vector.tensor_tensor(e_in[:, :, 2, :].rearrange(by_graph, c=2), d4, D4, ALU.subtract).then_inc(ein_done.sem, 1)
            if p1 is not None and s == 6:
                dve.wait_ge(e_done.sem, e_done.upto(p1, 2))
                nc.vector.tensor_scalar(a_neg[:, :, :], e_out[:, :, 0, :], -1.0, None, ALU.mult).then_inc(aneg_done.sem, 1)
            if p1 is not None and s in FACTORS:
                t = FACTORS.index(s)
                if t >= 2:
                    dve.wait_ge(x2_done.sem, x2_done.upto(p1, t - 1))
                dve.wait_ge(h1_done.sem, h1_done.upto(p1, t + 1))
                nc.vector.tensor_tensor(G[:, t % 2, 0, :, 0:OD], h1[:, t, :, :],
                                        e_out[:, t, 2, :].unsqueeze(2).broadcast_to([P, AH, OD]), ALU.mult)
                nc.vector.tensor_copy(G[:, t % 2, 0, :, OD:E1], e_out[:, t, 2, :].unsqueeze(2))
                nc.vector.tensor_copy(G[:, t % 2, 1, :, OD:E1], e_leak[:, t, :].unsqueeze(2)).then_inc(g1_done.sem, 1)
            if p1 is not None and 0 <= s - FIRST < EARLY:
                if s == FIRST:
                    dve.wait_ge(dneg_done.sem, dneg_done.upto(p1, 1))
                    dve.wait_ge(adjN_done.sem, adjN_done.upto(p1, 1))
                neighbours(s - FIRST, p1)
            if p1 is not None and s - 1 in FACTORS:
                t = FACTORS.index(s - 1)
                dve.wait_ge(x0_done.sem, x0_done.upto(p1, t + 1))
                flat = "p r h e -> p (r h e)"
                nc.vector.tensor_tensor(G[:, t % 2, :, :, :].rearrange(flat), G[:, t % 2, :, :, :].rearrange(flat),
                                        X[:, t, 0, :, :, :].rearrange(flat), ALU.subtract).then_inc(r_done.sem, 1)
            if p1 is not None and s == FIRST + 5:
                divide(0, p1, chain_d1)
        if p0 is not None:
            context_low(KC - 1)
        if p1 is not None:
            acc_leave(1, p1)
        for t in range(T):
            if p1 is not None and t == 3:
                neighbours(EARLY, p1)
            if p0 is not None:
                dve.wait_ge(use0.sem, use0.upto(p0, filled("D", t)))
                o = bank_of("D", t)
                if t == 0:
                    dve.wait_ge(xb_done.sem, xb_done.upto(p0, 1))
                if t == 0 and due(p0 - 1, T):
                    dve.wait_ge(hy_done.sem, hy_done.upto(p0 - 1, T))
                nc.vector.tensor_tensor(y[:, t, :], o[:, 0:H], xb[:, t, :], ALU.add).then_inc(y_done.sem, 1)

    def scalar_body(act, p0, p1, p2):
        flat = "p h e -> p (h e)"
        flat4 = "p r h e -> p (r h e)"
        if p2 is not None:
            chain_a2.start(p2)

        def context_high(c):
            act.wait_ge(pv_done.sem, pv_done.upto(p0, 4 * c + 4))
            nc.scalar.activation(cT_hi[:, c, :], ctx[:, :], ACT.Identity, bias=bv_c[:, c:c + 1]).then_inc(chi_done.sem, 1)

        if p0 is not None:
            for c in range(KC):
                act.wait_ge(use0.sem, use0.upto(p0, filled("A", c)))
                o = bank_of("A", c)
                nc.scalar.activation(hT_hi[:, c, :], o[:, :], ACT.Relu).then_inc(hi_done.sem, 1)
        for slot in range(SLOTS + 1):
            if p0 is not None and 0 <= slot - 1 < SLOTS:
                what, k = PROJECTIONS[slot - 1]
                act.wait_ge(use0.sem, use0.upto(p0, filled(what, k)))
                o = bank_of(what, k)
                if what == "Q":
                    nc.scalar.activation(qT[:, k, :], o[:, :], ACT.Identity, bias=bq8_c[:, k:k + 1],
                                         scale=float(HD) ** -0.5).then_inc(q_done.sem, 1)
                elif what == "K":
                    nc.scalar.activation(kT[:, k, :], o[:, :], ACT.Identity, bias=bk_c[:, k:k + 1]).then_inc(k_done.sem, 1)
                else:
                    nc.scalar.activation(v_sb[:, k, :], o[:, 0:H], ACT.Copy).then_inc(v_done.sem, 1)
            if p2 is not None and slot in (2, 7):
                tiles = (0, 1) if slot == 2 else (2, 3)
                for t in tiles:
                    act.wait_ge(v1_done.sem, v1_done.upto(p2, t + 1))
                    if t >= 2:
                        act.wait_ge(elu_done.sem, elu_done.upto(p2, t - 1))
                    elif due(p2 - 1, T):
                        act.wait_ge(elu_done.sem, elu_done.upto(p2 - 1, T))
                    last = nc.scalar.activation(e_sb[:, t % 2, :], h1[:, t, :, :].rearrange(flat), ACT.Relu, scale=-1.0)
                chain_a2.link(act, last, p2)
                for t in tiles:
                    nc.scalar.activation(e_sb[:, t % 2, :], e_sb[:, t % 2, :], ACT.Exp, scale=-1.0).then_inc(e1_done.sem, 1)
            if p1 is not None and slot == 6:
                act.wait_ge(rstd2_done.sem, rstd2_done.upto(p1, 1))
                if p0 is not None:
                    act.wait_ge(use0.sem, use0.upto(p0, filled("A", KC - 1)))
                for t in range(T):
                    nc.scalar.activation(hn[:, t, :], y[:, t, :], ACT.Identity, scale=rstd2[:, t:t + 1],
                                         bias=shift2[:, t:t + 1]).then_inc(ln2_done.sem, 1)
        if p1 is not None:
            for c in range(KC):
                act.wait_ge(e_filled.sem, e_filled.upto(p1, c + 1))
                o = bank_of("E", c)
                nc.scalar.activation(hT_hi[:, c, :], o[:, :], ACT.Relu).then_inc(hi2_done.sem, 1)
        for s in range(STEPS):
            if p0 is not None and 0 <= s - 1 < UNITS:
                n = s - 1
                act.wait_ge(rinv_done.sem, rinv_done.upto(p0, n + 1))
                nc.scalar.activation(probs[:, n % 4, 0, :], probs[:, n % 4, 0, :], ACT.Copy,
                                     scale=rinv[:, n % 4, 0:1]).then_inc(pn0_done.sem, 1)
            if p0 is not None and s in CONTEXT:
                context_high(CONTEXT.index(s))
            if p0 is not None and s < UNITS:
                o = bank_of("S", s)
                act.wait_ge(max_done.sem, max_done.upto(p0, s + 1))
                if s >= 4:
                    act.wait_ge(use0.sem, use0.upto(p0, filled("PT", s - 4)))
                elif due(p0 - 1, 1):
                    act.wait_ge(use0.sem, use0.upto(p0 - 1, filled("PT", UNITS - 1)))
                for q in range(2):
                    nc.scalar.activation(probs[:, s % 4, q, :], o[:, q * NODES:(q + 1) * NODES], ACT.Exp,
                                         bias=nmax[:, s % 4, q:q + 1],
                                         accum_out=rsum[:, s % 4, q:q + 1]).then_inc(exp_done.sem, 1)
            if p1 is not None and s < T:
                act.wait_ge(use1.sem, use1.upto(p1, filled("h", s)))
                o = bank_of("h", s)
                if s == 0 and due(p1 - 1, T):
                    act.wait_ge(elu_done.sem, elu_done.upto(p1 - 1, T))
                if s >= 2:
                    act.wait_ge(tw_done.sem, tw_done.upto(p1, s - 1))
                nc.scalar.activation(th[:, s % 2, :, :].rearrange(flat), o[:, 0:H], ACT.Tanh).then_inc(th_done.sem, 1)
                if s == 0 and due(p1 - 1, T):
                    act.wait_ge(out_done.sem, out_done.upto(p1 - 1, T))
                nc.scalar.activation(h1[:, s, :, :].rearrange(flat), o[:, 0:H], ACT.Copy).then_inc(h1_done.sem, 1)
            if p0 is not None and 0 <= s - 2 < UNITS:
                n = s - 2
                act.wait_ge(use0.sem, use0.upto(p0, filled("PT", n)))
                o = bank_of("PT", n)
                if n >= 3:
                    act.wait_ge(pv_done.sem, pv_done.upto(p0, n - 2))
                elif due(p0 - 1, UNITS):
                    act.wait_ge(pv_done.sem, pv_done.upto(p0 - 1, UNITS))
                nc.scalar.activation(probsT[:, n % 3, :, :].rearrange("p k q -> p (k q)"), o[:, :], ACT.Copy).then_inc(pt_done.sem, 1)
            if p1 is not None and s < 2:
                if s == 0:
                    act.wait_ge(ln2_done.sem, ln2_done.upto(p1, T))
                for t in (2 * s, 2 * s + 1):
                    nc.scalar.activation(hr[:, t, :], hn[:, t, :], ACT.Relu).then_inc(hr_done.sem, 1)
            if p1 is not None and 0 <= s - GATE - 1 < T:
                t = s - GATE - 1
                act.wait_ge(gl_done.sem, gl_done.upto(p1, t + 1))
                nc.scalar.activation(gl[:, t, :], gl[:, t, :], ACT.Tanh, scale=0.5).then_inc(gate_done.sem, 1)
            if p1 is not None and s == 4:
                act.wait_ge(adjT_in.sem, adjT_in.upto(p1, 16))
                if due(p1 - 1, UNITS):
                    act.wait_ge(mm_done.sem, mm_done.upto(p1 - 1, UNITS))
                nc.scalar.activation(adj_p[:, :, :], adjT_u[:, :, :], ACT.Copy).then_inc(adjT_done.sem, 1)
            if p1 is not None and s == 5:
                act.wait_ge(ein_done.sem, ein_done.upto(p1, 1))
                nc.scalar.activation(e_out[:, :, 0:2, :], e_in[:, :, 0:2, :], ACT.Exp)
                nc.scalar.activation(e_out[:, :, 2, :], e_in[:, :, 2, :], ACT.Exp, bias=shift_c[:, :]).then_inc(e_done.sem, 1)
                nc.scalar.activation(e_leak[:, :, :], e_in[:, :, 2, :], ACT.Exp, scale=LEAK, bias=shift_c[:, :]).then_inc(e_done.sem, 1)
            if p1 is not None and s - 1 in FACTORS:
                t = FACTORS.index(s - 1)
                act.wait_ge(r_done.sem, r_done.upto(p1, t + 1))
                nc.scalar.activation(X[:, t, 1, :, :, :].rearrange(flat4), G[:, t % 2, :, :, :].rearrange(flat4),
                                     ACT.Copy).then_inc(x1_done.sem, 1)
            if p1 is not None and s in FACTORS:
                t = FACTORS.index(s)
                act.wait_ge(g1_done.sem, g1_done.upto(p1, t + 1))
                act.wait_ge(g2_done.sem, g2_done.upto(p1, t + 1))
                nc.scalar.activation(X[:, t, 0, :, :, :].rearrange(flat4), G[:, t % 2, :, :, :].rearrange(flat4),
                                     ACT.Copy).then_inc(x0_done.sem, 1)
            if p1 is not None and s == FIRST - 2:
                act.wait_ge(use1.sem, use1.upto(p1, filled("sT", 0)))
                o = bank_of("sT", 0)
                nc.scalar.activation(sT[0:3 * AH, :], o[:, :].bitcast(BF16)[0:3 * AH, 0:W], ACT.Copy).then_inc(sT_done.sem, 1)
        if p0 is not None:
            context_high(KC - 1)

    def gpsimd_body(pool, pn, p0, p1, p2):
        flat = "p h e -> p (h e)"
        if pn is not None:
            chain_p0.start(pn)
        if p1 is not None:
            chain_p1.start(p1)

        def sum_parts(q, p):
            for i in range(2):
                pool.wait_ge(acc_out.sem, acc_out.upto(p, 2 * q + i + 1))
                nc.gpsimd.tensor_tensor(part1[:, i, :, :].rearrange(flat), part1[:, i, :, :].rearrange(flat),
                                        part2[:, i, :, :].rearrange(flat), ALU.add).then_inc(num_done.sem, 1)

        def add_bias(g, p):
            for t in (2 * g, 2 * g + 1):
                pool.wait_ge(f_done.sem, f_done.upto(p, 4 * g + 2 + t % 2 + 1))
                nc.gpsimd.tensor_tensor(h1[:, t, :, :], h1[:, t, :, :],
                                        gb_b[:, :].unsqueeze(1).broadcast_to([P, AH, OD]), ALU.add).then_inc(v1_done.sem, 1)

        for slot in range(SLOTS + 1):
            if p2 is not None and slot in (2, 5):
                sum_parts(slot // 3 + 2, p2)
            if p2 is not None and slot in (0, 6):
                add_bias(slot // 6, p2)
            if p0 is not None and slot == 0:
                pool.wait_ge(adj_in.sem, adj_in.upto(p0, 16))
                if due(p0 - 1, 1):
                    pool.wait_ge(use0.sem, use0.upto(p0 - 1, filled("S", UNITS - 1)))
                settle(pool)
                nc.gpsimd.tensor_scalar(mask[:, :, :], adj_u[:, :, :], -MASKED, MASKED, ALU.mult, ALU.add).then_inc(mask_done.sem, 1)
            if p1 is not None and slot == 3:
                pool.wait_ge(stat2_done.sem, stat2_done.upto(p1, 1))
                settle(pool)
                nc.gpsimd.tensor_scalar(negmean2[:, :], mv2[:, :, 0], -1.0, None, ALU.mult)
                chain_p1.link(pool, nc.gpsimd.tensor_scalar(veps2[:, :], mv2[:, :, 1], EPS, None, ALU.add), p1)
                chain_p1.link(pool, nc.gpsimd.tensor_tensor(rstd2[:, :], veps2[:, :], half[:, 0:T], ALU.pow), p1)
                nc.gpsimd.tensor_tensor(shift2[:, :], negmean2[:, :], rstd2[:, :], ALU.mult).then_inc(rstd2_done.sem, 1)
            if p2 is not None and slot in (4, 9):
                for t in ((0, 1) if slot == 4 else (2, 3)):
                    pool.wait_ge(elu_done.sem, elu_done.upto(p2, t + 1))
                    v = h1[:, t, :, :].rearrange(flat)
                    nc.gpsimd.tensor_tensor(v, v, hr[:, t, :], ALU.subtract).then_inc(w1_done.sem, 1)
            if p0 is not None and slot == 2:
                if due(p0 - 1, T):
                    pool.wait_ge(y_done.sem, y_done.upto(p0 - 1, T))
                pool.wait_ge(x_in.sem, x_in.upto(p0, 16))
                for t in range(T):
                    last = nc.gpsimd.tensor_tensor(xb[:, t, :], x_sb[:, t, :], bf_b[:, :], ALU.add)
                last.then_inc(xb_done.sem, 1)

        for s in range(STEPS):
            if pn is not None and s == 1:
                pool.wait_ge(stat_done.sem, stat_done.upto(pn, 1))
                settle(pool)
                chain_p0.link(pool, nc.gpsimd.tensor_scalar(veps[:, :], mv[:, :, 1], EPS, None, ALU.add), pn)
                nc.gpsimd.tensor_tensor(rstd[:, :], veps[:, :], half[:, 0:T], ALU.pow).then_inc(rstd_done.sem, 1)
            if p1 is not None and s < T:
                pool.wait_ge(th_done.sem, th_done.upto(p1, s + 1))
                if s == 0 and due(p1 - 1, T):
                    pool.wait_ge(x2_done.sem, x2_done.upto(p1 - 1, T))
                if s >= 2:
                    pool.wait_ge(sd_done.sem, sd_done.upto(p1, s - 1))
                th_f = th[:, s % 2, :, :].rearrange(flat)
                nc.gpsimd.tensor_tensor(tw[:, s % 2, 0:AH, :].rearrange(flat), th_f, wsrc_b[:, :], ALU.mult)
                nc.gpsimd.tensor_tensor(tw[:, s % 2, AH:2 * AH, :].rearrange(flat), th_f,
                                        wdst_b[:, :], ALU.mult).then_inc(tw_done.sem, 1)
            if p1 is not None and s == 4:
                pool.wait_ge(dm_done.sem, dm_done.upto(p1, 1))
                settle(pool)
                nc.gpsimd.partition_all_reduce(dmax[:, :], dmax2[:, :], P, bass.bass_isa.ReduceOp.max).then_inc(dmax_done.sem, 1)
            if p1 is not None and s in FACTORS:
                t = FACTORS.index(s)
                pool.wait_ge(e_done.sem, e_done.upto(p1, 2))
                pool.wait_ge(h1_done.sem, h1_done.upto(p1, t + 1))
                if t >= 2:
                    pool.wait_ge(x2_done.sem, x2_done.upto(p1, t - 1))
                nc.gpsimd.tensor_tensor(G[:, t % 2, 1, :, 0:OD], h1[:, t, :, :],
                                        e_leak[:, t, :].unsqueeze(2).broadcast_to([P, AH, OD]), ALU.mult).then_inc(g2_done.sem, 1)
            if p1 is not None and s - 1 in FACTORS:
                t = FACTORS.index(s - 1)
                f3 = "p r h e -> p (r h e)"
                pool.wait_ge(x1_done.sem, x1_done.upto(p1, t + 1))
                nc.gpsimd.tensor_tensor(X[:, t, 2, :, :, :].rearrange(f3), G[:, t % 2, :, :, :].rearrange(f3),
                                        X[:, t, 1, :, :, :].rearrange(f3), ALU.subtract).then_inc(x2_done.sem, 1)
            if p1 is not None and s == FACTORS[-1] + 2:
                pool.wait_ge(hr_done.sem, hr_done.upto(p1, T))
                for g in range(2):
                    if due(p1 - 1, 16):
                        pool.wait_ge(stored[g].sem, stored[g].upto(p1 - 1, 16))
                for t in range(T):
                    nc.gpsimd.tensor_tensor(hy[:, t, :], hr[:, t, :], y[:, t, :], ALU.add).then_inc(hy_done.sem, 1)
            if p1 is not None and s == FIRST + 4:
                sum_parts(0, p1)
        if p1 is not None:
            sum_parts(1, p1)

    shift_c = sb("shift_c", [P, 1])
    block = nc.Block()
    with block:
        @block.sync
        def _(sp):
            sp.dma_start(x_sb[:, :, :], x_v[0, :, :, :]).then_inc(x_in.sem, 16)
            sp.dma_start(adj_u[:, :, :], adj_v[0, :, :, :]).then_inc(adj_in.sem, 16)
            sp.dma_start(stage[0], w_dram[0].rearrange("(c p) n -> p c n", p=P)).then_inc(w_in[0].sem, 16)
            for col, dst in ((bq, bq_c), (bk, bk_c), (bv, bv_c)):
                sp.dma_start(dst[:, :], col).then_inc(rows_in.sem, 16)
            for row, dst in ((bf, bf_b), (Hb, Hb_b), (w_src, wsrc_b), (w_dst, wdst_b), (gb, gb_b)):
                sp.dma_start(dst[:, :], row.partition_broadcast(P).rearrange("p a n -> p (a n)")).then_inc(rows_in.sem, 16)
            for n in range(1, len(w_names)):
                sp.dma_start(stage[n], w_dram[n].rearrange("(c p) n -> p c n", p=P)).then_inc(w_in[n].sem, 16)
            sync_body(sp, 1, 0, None, None)
            sync_body(sp, 2, 1, 0, None)
            sync_body(sp, 3, 2, 1, 0)
            with sp.Fori(3, PAIRS - 1) as i:
                sync_body(sp, i + 1, i, i - 1, i - 2)
            sync_body(sp, None, PAIRS - 1, PAIRS - 2, PAIRS - 3)
            sync_body(sp, None, None, PAIRS - 1, PAIRS - 2)
            sync_body(sp, None, None, None, PAIRS - 1)
            for g in range(2):
                sp.wait_ge(stored[g].sem, stored[g].upto(PAIRS, 0))

        @block.tensor
        def _(pe):
            pe.wait_ge(consts.sem, 3)
            tensor_body(pe, 0, None, None)
            tensor_body(pe, 1, 0, None)
            tensor_body(pe, 2, 1, 0)
            with pe.Fori(3, PAIRS) as i:
                tensor_body(pe, i, i - 1, i - 2)
            tensor_body(pe, None, PAIRS - 1, PAIRS - 2)
            tensor_body(pe, None, None, PAIRS - 1)

        @block.vector
        def _(dve):
            nc.vector.memset(shift_c[:, :], SHIFT).then_inc(consts.sem, 1)
            vector_body(dve, 0, None, None, None)
            for n, name in enumerate(w_names):
                dve.wait_ge(w_hi_done.sem, n + 1)
                nc.vector.tensor_tensor(w_lo[name][:, :, :], stage[n], w_hi[name][:, :, :].bitcast(F32),
                                        ALU.subtract).then_inc(w_lo_done.sem, 1)
            dve.wait_ge(rows_in.sem, 16 * 8)
            nc.vector.tensor_scalar(bq8_c[:, :], bq_c[:, :], float(HD) ** -0.5, None, ALU.mult).then_inc(consts.sem, 1)
            vector_body(dve, 1, 0, None, None)
            vector_body(dve, 2, 1, 0, None)
            vector_body(dve, 3, 2, 1, 0)
            with dve.Fori(3, PAIRS - 1) as i:
                vector_body(dve, i + 1, i, i - 1, i - 2)
            vector_body(dve, None, PAIRS - 1, PAIRS - 2, PAIRS - 3)
            vector_body(dve, None, None, PAIRS - 1, PAIRS - 2)
            vector_body(dve, None, None, None, PAIRS - 1)

        @block.scalar
        def _(act):
            for n, name in enumerate(w_names):
                act.wait_ge(w_in[n].sem, 16)
                nc.scalar.activation(w_hi[name][:, :, :], stage[n], ACT.Copy).then_inc(w_hi_done.sem, 1)
            act.wait_ge(rows_in.sem, 16 * 8)
            act.wait_ge(consts.sem, 3)
            scalar_body(act, 0, None, None)
            scalar_body(act, 1, 0, None)
            scalar_body(act, 2, 1, 0)
            with act.Fori(3, PAIRS) as i:
                scalar_body(act, i, i - 1, i - 2)
            scalar_body(act, None, PAIRS - 1, PAIRS - 2)
            scalar_body(act, None, None, PAIRS - 1)

        @block.gpsimd
        def _(pool):
            set_up = nc.alloc_semaphore("set_up")
            nc.gpsimd.memset(half[:, :], -0.5).then_inc(set_up, 1)
            nc.gpsimd.memset(ident[:, :], 0.0).then_inc(set_up, 1)
            nc.gpsimd.memset(sel[:, :, :], 0.0).then_inc(set_up, 1)
            nc.gpsimd.memset(sT[:, :], 0.0).then_inc(set_up, 1)
            pool.wait_ge(set_up, 4)
            nc.gpsimd.affine_select(out=ident[:, :], in_=ident[:, :], compare_op=ALU.not_equal, fill=1.0, base=0,
                                    pattern=[[-1, P]], channel_multiplier=1).then_inc(set_up, 1)
            pool.wait_ge(set_up, 5)
            nc.gpsimd.tensor_copy(ident_b[:, :], ident[:, :]).then_inc(set_up, 1)
            for j in range(3):
                nc.gpsimd.affine_select(out=sel[:, :, :], in_=sel[:, :, :], compare_op=ALU.not_equal, fill=1.0,
                                        base=-AH * j, pattern=[[-1, AH], [0, P]], channel_multiplier=1).then_inc(set_up, 1)
                pool.wait_ge(set_up, 7 + j)
            pool.wait_ge(rows_in.sem, 16 * 8)
            pool.nop().then_inc(consts.sem, 1)
            gpsimd_body(pool, 0, None, None, None)
            gpsimd_body(pool, 1, 0, None, None)
            gpsimd_body(pool, 2, 1, 0, None)
            gpsimd_body(pool, 3, 2, 1, 0)
            with pool.Fori(3, PAIRS - 1) as i:
                gpsimd_body(pool, i + 1, i, i - 1, i - 2)
            gpsimd_body(pool, None, PAIRS - 1, PAIRS - 2, PAIRS - 3)
            gpsimd_body(pool, None, None, PAIRS - 1, PAIRS - 2)
            gpsimd_body(pool, None, None, None, PAIRS - 1)


_INS = ["x", "adj", "adjT", "Wq", "Wk", "Wv", "Wf", "W1", "HwT", "bq", "bk", "bv", "bf", "gb", "w_src", "w_dst", "Hb"]


def kernel(**inputs):
    import numpy as np
    import concourse.bacc as bacc
    from concourse.bass_utils import run_bass_kernel_spmd

    a = {k: np.asarray(v) for k, v in inputs.items()}
    adj = a["adj"]
    laid = {
        "x": a["x"], "adj": adj, "adjT": adj.transpose(0, 2, 1),
        "Wq": a["L0_gnn_Wq"], "Wk": a["L0_gnn_Wk"], "Wv": a["L0_gnn_Wv"], "Wf": a["L0_gnn_Wf"],
        "W1": a["L1_gnn_W"].transpose(1, 0, 2).reshape(H, H), "HwT": a["L1_gnn_H_w"].T,
        "bq": a["L0_gnn_bq"].reshape(KC, P).T, "bk": a["L0_gnn_bk"].reshape(KC, P).T, "bv": a["L0_gnn_bv"].reshape(KC, P).T, "bf": a["L0_gnn_bf"][None],
        "gb": a["L1_gnn_b"][None], "w_src": a["L1_gnn_w_src"].reshape(1, H), "w_dst": a["L1_gnn_w_dst"].reshape(1, H),
        "Hb": a["L1_gnn_H_b"][None],
    }
    nc = bacc.Bacc("TRN2", target_bir_lowering=False, num_devices=1)
    arrays, args = {}, []
    for name in _INS:
        v = np.ascontiguousarray(laid[name])
        arrays[f"in_{name}"] = v
        args.append(nc.dram_tensor(f"in_{name}", v.shape, mybir.dt.from_np(v.dtype), kind="ExternalInput").ap())
    args.append(nc.dram_tensor("out", (GRAPHS, NODES, H), F32, kind="ExternalOutput").ap())
    graph_layers(nc, *args)
    r = run_bass_kernel_spmd(nc, [arrays], core_ids=[0])
    return r.results[0]["out"]
```

```python
import concourse.bass as bass
from concourse import mybir

F32 = mybir.dt.float32
F32R = mybir.dt.float32r
BF16 = mybir.dt.bfloat16
U8 = mybir.dt.uint8
ALU = mybir.AluOpType
ACT = mybir.ActivationFunctionType
AX = mybir.AxisListType

P = 128
GRAPHS, NODES, H = 32, 256, 384
PAIRS = GRAPHS // 2
T = 2 * NODES // P
W = T * P
KC = H // P
NH, HD = 6, 64
AH, OD = 12, 32
E1 = OD + 1
UNITS = 2 * NH
SLOTS = 10
PROJECTIONS = [("Q", c) for c in range(KC)] + [("K", c) for c in range(KC)] + [("V", t) for t in range(T)]
STEPS = UNITS + 3
FIRST = 9
EARLY = STEPS - FIRST
H_STEPS, GATE_STEPS = ((0, 0, 1, 1), (2, 3, 4, 5))
SD_STEPS = (1, 1, 2, 3)
PREPARE = 3
S_STEP = 7
FACTORS = (5, 7, 9, 11)
MIDDLE = 1
HY_STEP = 12
CONTEXT = (7, 11)
LATER = (4, 8)
NORM = 13
STATS_SLOT, NORM_SLOT = (3, 5)
NEXT_SLOT, ADJ_SLOT = (7, 8)
EXP_SLOTS, ELU_SLOTS, MIX_SLOT = ((4, 8), (4, 9), 6)
LEAVE = tuple(min(FIRST + 2 + n, STEPS) if n < EARLY else FIRST + 1 + n for n in (2, 5, 8, 11))
DIVIDE = tuple(n + 1 + (n + 1 == STEPS) for n in LEAVE)


def at(steps, s):
    return [n for n, step in enumerate(steps) if step == s]


EPS = 1e-5
MASKED = -9000000000000000.0
LEAK = 0.2
SHIFT = 40.0

def unit(n):
    c, g, side = n // 4, (n // 2) % 2, n % 2
    return c, g, side, 2 * c + side


class Signal:

    def __init__(self, nc, name, per):
        self.sem, self.per = nc.alloc_semaphore(name), per

    def upto(self, p, k):
        return p * self.per + k


def due(p, k):
    return not isinstance(p, int) or p > 0 or (p == 0 and k > 0)


class Chain:

    def __init__(self, nc, name):
        self.sem, self.per, self.count = nc.alloc_semaphore(name), None, 0

    def start(self, p):
        if self.per is None and self.count:
            self.per = self.count
        assert isinstance(p, int) and p == 0 or self.per is not None
        self.count = 0

    def link(self, eng, ins, p):
        self.count += 1
        ins.then_inc(self.sem, 1)
        eng.wait_ge(self.sem, (0 if isinstance(p, int) and p == 0 else p * self.per) + self.count)


def _banks():
    layer0 = [("A", c) for c in range(KC)] + PROJECTIONS + [("E", c) for c in range(KC)]
    for s in range(UNITS + 2):
        layer0 += [("S", s)] * (s < UNITS) + [("PT", s - 2)] * (s >= 2)
    layer0 += [("D", t) for t in range(T)]
    layer0 = [(x, n % 3) for n, x in enumerate(layer0)]
    layer1 = []
    for s in range(STEPS):
        layer1 += [("h", t) for t in at(H_STEPS, s)] + [("gate", t) for t in at(GATE_STEPS, s)]
    layer1 += [("sT", 0)]
    layer1 = [(x, 4 + n % 4) for n, x in enumerate(layer1)]
    layer1 += [(("SR", n), 4 + (n + 1) % 2) for n in range(UNITS)]
    uses, totals = {}, []
    for lot in (layer0, layer1):
        last, count = {}, 0
        for x, b in lot:
            uses[x] = (b, count, last.get(b, ()))
            last[b] = (x, *last.get(b, ()))
            count += x[0] != "E"
        for x, (b, n, earlier) in list(uses.items()):
            if not earlier:
                uses[x] = (b, n, (last.get(b, ((None, 0),))[0], "pair before"))
        totals.append(count)
    return uses, totals[0], totals[1]


USES, USES0, USES1 = _banks()


def graph_layers(nc, x, adj, adjT, Wq, Wk, Wv, Wf, W1, HwT, bq, bk, bv, bf, gb, w_src, w_dst, Hb, out):
    x_v = x.rearrange("(a g) (c q) f -> a q (g c) f", g=2, q=P)
    adj_v = adj.rearrange("(a g) (c q) k -> a q (g c) k", g=2, q=P)
    adjT_v = adjT.rearrange("(a g) (c q) k -> a q (g c) k", g=2, q=P)
    out_v = out.rearrange("(a g) (c q) f -> a q (g c) f", g=2, q=P)

    def sb(name, shape, dt=F32):
        return nc.alloc_sbuf_tensor(name, shape, dt)

    w_names = ("Wq", "Wk", "Wv", "Wf", "W1", "Hw")
    w_dram = (Wq, Wk, Wv, Wf, W1, HwT)
    w_hi = {n: sb(n + "_hi", [P, KC, H], F32R) for n in w_names}
    w_lo = {n: sb(n + "_lo", [P, KC, H], F32R) for n in w_names}
    bf_b, Hb_b = sb("bf_b", [P, H]), sb("Hb_b", [P, H])
    wsrc_b, wdst_b, gb_b = sb("wsrc_b", [P, H]), sb("wdst_b", [P, H]), sb("gb_b", [P, OD])
    bq_c, bq8_c, bk_c, bv_c = sb("bq_c", [P, KC]), sb("bq8_c", [P, KC]), sb("bk_c", [P, KC]), sb("bv_c", [P, KC])
    ident = sb("ident", [P, P])
    ident_b = sb("ident_b", [P, P], BF16)
    sel = sb("sel", [P, AH, P], BF16)
    half = sb("half", [P, 2 * T])
    x_sb, xb = sb("x_sb", [P, T, H]), sb("xb", [P, T, H])
    adj_u = sb("adj_u", [P, T, NODES], U8)
    mask = sb("mask", [P, T, NODES], BF16)
    stats, mv, rstd, veps = sb("stats", [P, T, 6]), sb("mv", [P, T, 2]), sb("rstd", [P, T]), sb("veps", [P, T])
    hn = sb("hn", [P, T, H])
    hT_hi, hT_lo = sb("hT_hi", [P, KC, W], F32R), sb("hT_lo", [P, KC, W], F32R)
    qT, kT, v_sb = sb("qT", [P, KC, W]), sb("kT", [P, KC, W]), sb("v_sb", [P, T, H])
    probs = sb("probs", [P, 4, 2, NODES])
    probsT = sb("probsT", [P, 3, 2, NODES])
    nmax, rsum, rinv = sb("nmax", [P, 4, 2]), sb("rsum", [P, 4, 2]), sb("rinv", [P, 4, 2])
    y = sb("y", [P, T, H])
    adjT_u = sb("adjT_u", [P, T, NODES], U8)
    adj_p, adj_n = sb("adj_p", [P, T, NODES], BF16), sb("adj_n", [P, T, NODES], BF16)
    stats2, mv2, rstd2, veps2 = sb("stats2", [P, T, 6]), sb("mv2", [P, T, 2]), sb("rstd2", [P, T]), sb("veps2", [P, T])
    negmean, shift1 = sb("negmean", [P, T]), sb("shift1", [P, T])
    negmean2, shift2 = sb("negmean2", [P, T]), sb("shift2", [P, T])
    hr, hy = sb("hr", [P, T, H]), sb("hy", [P, T, H])
    h1 = sb("h1", [P, T, AH, OD])
    gl = sb("gl", [P, T, H])
    sd = sb("sd", [P, T, 2 * AH])
    dmax2, dmax = sb("dmax2", [P, 2 * AH]), sb("dmax", [P, 2 * AH])
    s_rest = sb("s_rest", [P, T, AH])
    s_parts = sb("s_parts", [P, T, 3 * AH], BF16)
    sT = sb("sT", [P, W], BF16)
    d_neg = sb("d_neg", [P, T, AH])
    u_sb, m_sb = sb("u_sb", [P, T, AH]), sb("m_sb", [P, T, AH])
    e_in, e_out = sb("e_in", [P, T, 3, AH]), sb("e_out", [P, T, 3, AH])
    e_leak = sb("e_leak", [P, T, AH])
    a_neg = sb("a_neg", [P, T, AH])
    G = sb("G", [P, 2, 2, AH, E1])
    g_flat = G[:, :, :, :, :].rearrange("p s r h e -> p (s r h e)")
    tw = g_flat[:, 0:4 * H].rearrange("p (s h e) -> p s h e", s=2, e=OD)
    stage = [y[:, 0:KC, :], hr[:, 0:KC, :], hy[:, 0:KC, :], gl[:, 0:KC, :], h1[:, 0:KC, :, :].rearrange("p c h e -> p c (h e)"),
             g_flat[:, 0:KC * H].rearrange("p (c n) -> p c n", c=KC)]
    X = sb("X", [P, T, 3, 2, AH, E1], BF16)
    Mp = sb("Mp", [P, 2, 2, 2, NODES], BF16)
    part1, part2 = sb("part1", [P, 2, NH, E1]), sb("part2", [P, 2, NH, E1])
    dinv = sb("dinv", [P, 2, NH])
    e_sb = sb("e_sb", [P, 2, H])
    th = e_sb[:, :, :].rearrange("p s (h e) -> p s h e", e=OD)
    cT_hi, cT_lo = hT_hi, hT_lo

    bank = [nc.alloc_psum_tensor(f"bank{b}", [P, 512], F32) for b in range(8)]
    ctx = bank[3]
    acc = [bank[6], bank[7]]

    def sig(name, per):
        return Signal(nc, name, per)

    w_in = [sig("w_in_" + n, 0) for n in w_names]
    w_hi_done, w_lo_done = sig("w_hi_done", 0), sig("w_lo_done", 0)
    rows_in, consts = sig("rows_in", 0), sig("consts", 0)
    sel_done = nc.alloc_semaphore("sel_done")
    x_in, adj_in, adjT_in = sig("x_in", 16), sig("adj_in", 16), sig("adjT_in", 16)
    use0, use1 = sig("use0", USES0), sig("use1", USES1)
    stat_done, rstd_done, ln1_done = sig("stat_done", 1), sig("rstd_done", 1), sig("ln1_done", T)
    xb_done, mask_done = sig("xb_done", 1), sig("mask_done", 1)
    hi_done, lo_done = sig("hi_done", KC), sig("lo_done", KC)
    e_filled = sig("e_filled", KC)
    q_done, k_done, v_done = sig("q_done", KC), sig("k_done", KC), sig("v_done", T)
    max_done, exp_done, rinv_done = sig("max_done", UNITS), sig("exp_done", 2 * UNITS), sig("rinv_done", UNITS)
    pn0_done, pn1_done = sig("pn0_done", UNITS), sig("pn1_done", UNITS)
    pt_done, pv_done = sig("pt_done", UNITS), sig("pv_done", UNITS)
    chi_done, clo_done, y_done = sig("chi_done", KC), sig("clo_done", KC), sig("y_done", T)
    adjT_done, adjN_done = sig("adjT_done", 1), sig("adjN_done", 1)
    stat2_done, rstd2_done, ln2_done = sig("stat2_done", 1), sig("rstd2_done", 1), sig("ln2_done", T)
    hr_done, hy_done = sig("hr_done", T), sig("hy_done", T)
    hi2_done, lo2_done = sig("hi2_done", KC), sig("lo2_done", KC)
    th_done, h1_done, gl_done, gate_done = sig("th_done", T), sig("h1_done", T), sig("gl_done", T), sig("gate_done", T)
    tw_done, sd_done, dm_done, dmax_done = sig("tw_done", T), sig("sd_done", T), sig("dm_done", 1), sig("dmax_done", 1)
    parts_done, sT_done = sig("parts_done", 1), sig("sT_done", 1)
    ein_done, e_done, dneg_done, aneg_done = sig("ein_done", 1), sig("e_done", 2), sig("dneg_done", 1), sig("aneg_done", 1)
    g1_done, g2_done = sig("g1_done", T), sig("g2_done", T)
    x0_done, r_done, x1_done, x2_done = sig("x0_done", T), sig("r_done", T), sig("x1_done", T), sig("x2_done", T)
    m_done, mm_done = sig("m_done", UNITS), sig("mm_done", UNITS)
    acc_out, num_done, f_done, v1_done = sig("acc_out", 2 * T), sig("num_done", 2 * T), sig("f_done", 2 * T), sig("v1_done", T)
    e1_done, elu_done, w1_done, out_done, stored = (sig("e1_done", T), sig("elu_done", T), sig("w1_done", T),
                                                   sig("out_done", T), [sig("stored01", 16), sig("stored23", 16)])
    chain_d0, chain_d1 = Chain(nc, "chain_d0"), Chain(nc, "chain_d1")
    chain_p0, chain_p1 = Chain(nc, "chain_p0"), Chain(nc, "chain_p1")
    chain_a2, chain_d2 = Chain(nc, "chain_a2"), Chain(nc, "chain_d2")

    def bank_of(name, k):
        return bank[USES[name, k][0]]

    def filled(name, k):
        return USES[name, k][1] + 1

    def read(name, k):
        return {
            "A": (lo_done, k + 1), "Q": (q_done, k + 1), "K": (k_done, k + 1), "V": (v_done, k + 1),
            "S": (exp_done, 2 * k + 2), "PT": (pt_done, k + 1), "D": (y_done, k + 1),
            "E": (lo2_done, k + 1), "h": (h1_done, k + 1), "gate": (gl_done, k + 1), "sT": (sT_done, 1),
            "SR": (m_done, k + 1), "acc": (acc_out, 2 * T),
        }[name]

    def before(p, name, k):
        b, _, earlier = USES[name, k]
        if earlier[1:] == ("pair before",):
            what = ("acc", 0) if b in (6, 7) else earlier[0]
            return (*read(*what), p - 1)
        if earlier[0][0] == "E":
            return (*read(*earlier[1]), p) if isinstance(p, int) and p == 0 else (*read(*earlier[0]), p - 1)
        return (*read(*earlier[0]), p)

    def used_before(p, name, k):
        signal, count, pair = before(p, name, k)
        return due(pair, count)

    def reader_done(p, name, k):
        signal, count, pair = before(p, name, k)
        return signal.sem, signal.upto(pair, count)

    def seg(n):
        return slice(n * P, (n + 1) * P)

    def gat(n):
        return n // 6, 2 * (n % 6)

    waited = nc.alloc_semaphore("waited")

    def settle(eng):
        eng.sem_inc(waited, 1)

    def sync_body(sp, pn, p0, p1, p2):
        if pn is not None:
            if due(pn - 1, 1):
                sp.wait_ge(ln1_done.sem, ln1_done.upto(pn - 1, T))
                settle(sp)
                sp.wait_ge(xb_done.sem, xb_done.upto(pn - 1, 1))
                settle(sp)
            sp.dma_start(x_sb[:, :, :], x_v[pn, :, :, :]).then_inc(x_in.sem, 16)
            if due(pn - 1, 1):
                sp.wait_ge(mask_done.sem, mask_done.upto(pn - 1, 1))
                settle(sp)
            sp.dma_start(adj_u[:, :, :], adj_v[pn, :, :, :]).then_inc(adj_in.sem, 16)
        if p2 is not None:
            for g in range(2):
                sp.wait_ge(out_done.sem, out_done.upto(p2, 2 * g + 2))
                settle(sp)
                sp.dma_start(out_v[p2, :, 2 * g:2 * g + 2, :],
                             hy[:, 2 * g:2 * g + 2, :]).then_inc(stored[g].sem, 16)
        if p0 is not None:
            if due(p0 - 1, 2):
                sp.wait_ge(adjT_done.sem, adjT_done.upto(p0 - 1, 1))
                settle(sp)
                sp.wait_ge(adjN_done.sem, adjN_done.upto(p0 - 1, 1))
                settle(sp)
            sp.dma_start(adjT_u[:, :, :], adjT_v[p0, :, :, :]).then_inc(adjT_in.sem, 16)

    def chunk_product(o, c, stat_hi, stat_lo, mov_hi, mov_lo):
        nc.tensor.matmul(o, stat_hi, mov_hi, start=c == 0, stop=False, skip_group_check=True)
        nc.tensor.matmul(o, stat_hi, mov_lo, start=False, stop=False, skip_group_check=True)
        return nc.tensor.matmul(o, stat_lo, mov_hi, start=False, stop=c == KC - 1, skip_group_check=True)

    def project_T(o, name, k, c):
        return chunk_product(o[:, :], c, w_hi[name][:, c, seg(k)], w_lo[name][:, c, seg(k)], hT_hi[:, c, :], hT_lo[:, c, :])

    def project(o, name, t, c):
        return chunk_product(o[:, 0:H], c, hT_hi[:, c, seg(t)], hT_lo[:, c, seg(t)], w_hi[name][:, c, :], w_lo[name][:, c, :])

    def tensor_body(pe, p0, p1, p2):
        def s_rows(n, p):
            g, head = gat(n)
            if used_before(p, "SR", n):
                pe.wait_ge(*reader_done(p, "SR", n))
            o = bank_of("SR", n)
            for k in range(2):
                last = nc.tensor.matmul(o[:, k * NODES:(k + 1) * NODES], sel[:, head + k, :],
                                        sT[:, g * NODES:(g + 1) * NODES], start=True, stop=True)
            last.then_inc(use1.sem, 1)

        def gather(n, p):
            g, head = gat(n)
            first = head - head % NH
            if n == 0:
                pe.wait_ge(adjT_done.sem, adjT_done.upto(p, 1))
                pe.wait_ge(gl_done.sem, gl_done.upto(p, T))
                pe.wait_ge(h1_done.sem, h1_done.upto(p, T))
            elif n % 3 == 0:
                pe.wait_ge(acc_out.sem, acc_out.upto(p, 2 * (n // 3)))
            if n % 6 == 0:
                pe.wait_ge(x2_done.sem, x2_done.upto(p, 2 * g + 2))
            if n % 3 == 0:
                for i in range(2):
                    for j in range(2):
                        for part in range(3):
                            nc.tensor.matmul(acc[i][:, NH * E1:2 * NH * E1], adj_p[:, 2 * g + j, seg(i)],
                                             X[:, 2 * g + j, part, 1, first:first + NH, :],
                                             start=j == 0 and part == 0, stop=False, skip_group_check=True)
            pe.wait_ge(m_done.sem, m_done.upto(p, n + 1))
            for k in range(2):
                col = (head + k) % NH
                for i in range(2):
                    o = acc[i][:, 0:2 * NH * E1].rearrange("p (r h e) -> p r h e", r=2, h=NH)[:, :, col, :]
                    for j in range(2):
                        for part in range(3):
                            last = nc.tensor.matmul(o, Mp[:, n % 2, k, j, seg(i)], X[:, 2 * g + j, part, :, head + k, :],
                                                    start=False, stop=False, skip_group_check=True)
            last.then_inc(mm_done.sem, 1)

        def scores(n):
            c, g, side, head = unit(n)
            rows = slice(side * HD, (side + 1) * HD)
            if used_before(p0, "S", n):
                pe.wait_ge(*reader_done(p0, "S", n))
            o = bank_of("S", n)
            if n == 0:
                pe.wait_ge(q_done.sem, q_done.upto(p0, KC))
                pe.wait_ge(k_done.sem, k_done.upto(p0, KC))
                pe.wait_ge(mask_done.sem, mask_done.upto(p0, 1))
            for q in range(2):
                t = 2 * g + q
                o_q = o[:, q * NODES:(q + 1) * NODES]
                nc.tensor.matmul(o_q, qT[rows, c, seg(t)], kT[rows, c, g * NODES:(g + 1) * NODES], start=True, stop=False)
                last = nc.tensor.matmul(o_q, ident_b[:, :], mask[:, t, :], start=False, stop=True)
            last.then_inc(use0.sem, 1)

        def probs_T(n):
            if used_before(p0, "PT", n):
                pe.wait_ge(*reader_done(p0, "PT", n))
            o = bank_of("PT", n)
            for q in range(2):
                normalised = (pn0_done, pn1_done)[q]
                pe.wait_ge(normalised.sem, normalised.upto(p0, n + 1))
                for k in range(2):
                    last = nc.tensor.transpose(o[:, k * NODES + q * P:k * NODES + (q + 1) * P],
                                               probs[:, n % 4, q, seg(k)], ident[:, :])
            last.then_inc(use0.sem, 1)

        def context(n):
            c, g, side, head = unit(n)
            pe.wait_ge(pt_done.sem, pt_done.upto(p0, n + 1))
            if n == 0:
                pe.wait_ge(v_done.sem, v_done.upto(p0, T))
            if n == 0 and due(p0 - 1, KC):
                pe.wait_ge(clo_done.sem, clo_done.upto(p0 - 1, KC))
            if n % 4 == 0 and c > 0:
                pe.wait_ge(clo_done.sem, clo_done.upto(p0, c))
            for k in range(2):
                last = nc.tensor.matmul(ctx[side * HD:(side + 1) * HD, g * NODES:(g + 1) * NODES],
                                        v_sb[:, 2 * g + k, head * HD:(head + 1) * HD], probsT[:, n % 3, k, :],
                                        start=k == 0, stop=k == 1)
            last.then_inc(pv_done.sem, 1)

        if p2 is not None:
            s_rows(EARLY + 1, p2)
        if p0 is not None:
            for c in range(KC):
                if used_before(p0, "A", c):
                    pe.wait_ge(*reader_done(p0, "A", c))
                o = bank_of("A", c)
                for t in range(T):
                    if c == 0:
                        pe.wait_ge(ln1_done.sem, ln1_done.upto(p0, t + 1))
                    last = nc.tensor.transpose(o[:, seg(t)], hn[:, t, seg(c)], ident[:, :])
                last.then_inc(use0.sem, 1)
        if p2 is not None:
            gather(EARLY, p2)
        for slot in range(SLOTS):
            n = EARLY + 1 + slot
            if p2 is not None and n + 1 < UNITS:
                s_rows(n + 1, p2)
            if p0 is not None:
                what, k = PROJECTIONS[slot]
                if isinstance(p0, int) and p0 == 0:
                    pe.wait_ge(w_lo_done.sem, w_names.index("W" + what.lower()) + 1)
                if used_before(p0, what, k):
                    pe.wait_ge(*reader_done(p0, what, k))
                o = bank_of(what, k)
                for c in range(KC):
                    if slot == 0:
                        pe.wait_ge(hi_done.sem, hi_done.upto(p0, c + 1))
                        pe.wait_ge(lo_done.sem, lo_done.upto(p0, c + 1))
                    if what == "V":
                        last = project(o, "Wv", k, c)
                    else:
                        last = project_T(o, {"Q": "Wq", "K": "Wk"}[what], k, c)
                last.then_inc(use0.sem, 1)
            if p2 is not None and n < UNITS:
                gather(n, p2)
        if p1 is not None:
            for c in range(KC):
                if p0 is not None:
                    pe.wait_ge(*reader_done(p0, "E", c))
                o = bank_of("E", c)
                for t in range(T):
                    if c == 0:
                        pe.wait_ge(ln2_done.sem, ln2_done.upto(p1, t + 1))
                    last = nc.tensor.transpose(o[:, seg(t)], hn[:, t, seg(c)], ident[:, :])
                last.then_inc(e_filled.sem, 1)
        for s in range(STEPS):
            if p0 is not None and s < UNITS:
                scores(s)
            for what, name, t in [("h", "W1", t) for t in at(H_STEPS, s)] + [("gate", "Hw", t) for t in at(GATE_STEPS, s)]:
                if p1 is not None:
                    if used_before(p1, what, t):
                        pe.wait_ge(*reader_done(p1, what, t))
                    for c in range(KC):
                        if t == 0 and what == "h":
                            pe.wait_ge(hi2_done.sem, hi2_done.upto(p1, c + 1))
                            pe.wait_ge(lo2_done.sem, lo2_done.upto(p1, c + 1))
                        last = project(bank_of(what, t), name, t, c)
                    last.then_inc(use1.sem, 1)
            if p0 is not None and 0 <= s - 2 < UNITS:
                probs_T(s - 2)
            if p1 is not None and s == S_STEP:
                if used_before(p1, "sT", 0):
                    pe.wait_ge(*reader_done(p1, "sT", 0))
                pe.wait_ge(parts_done.sem, parts_done.upto(p1, 1))
                settle(pe)
                o_b = bank_of("sT", 0)[:, :].bitcast(BF16)
                for t in range(T):
                    last = nc.tensor.transpose(o_b[0:3 * AH, seg(t)], s_parts[:, t, :], ident_b[:, :])
                last.then_inc(use1.sem, 1)
            if p1 is not None and s == FIRST:
                pe.wait_ge(sT_done.sem, sT_done.upto(p1, 1))
            if p1 is not None and 0 <= s - FIRST < EARLY:
                s_rows(s - FIRST, p1)
            if p0 is not None and 0 <= s - 3 < UNITS and s - 3 not in LATER:
                if s - 4 in LATER:
                    context(s - 4)
                context(s - 3)
            if p1 is not None and 0 <= s - FIRST - 1 < EARLY - 1:
                gather(s - FIRST - 1, p1)
        def output(t, chunks):
            for c in chunks:
                last = project(bank_of("D", t), "Wf", t, c)
            return last

        if p1 is not None:
            s_rows(EARLY, p1)
        if p0 is not None:
            if isinstance(p0, int) and p0 == 0:
                pe.wait_ge(w_lo_done.sem, len(w_names))
            pe.wait_ge(chi_done.sem, chi_done.upto(p0, KC - 1))
            pe.wait_ge(clo_done.sem, clo_done.upto(p0, KC - 1))
            for t in range(3):
                if used_before(p0, "D", t):
                    pe.wait_ge(*reader_done(p0, "D", t))
                output(t, range(KC - 1))
        if p1 is not None:
            gather(EARLY - 1, p1)
        if p0 is not None:
            pe.wait_ge(chi_done.sem, chi_done.upto(p0, KC))
            pe.wait_ge(clo_done.sem, clo_done.upto(p0, KC))
            for t in range(3):
                output(t, [KC - 1]).then_inc(use0.sem, 1)
            for t in range(3, T):
                pe.wait_ge(*reader_done(p0, "D", t))
                output(t, range(KC)).then_inc(use0.sem, 1)

    def weights_low(first, end):
        for n in range(first, end):
            nc.vector.wait_ge(w_hi_done.sem, n + 1)
            nc.vector.tensor_tensor(w_lo[w_names[n]][:, :, :], stage[n], w_hi[w_names[n]][:, :, :].bitcast(F32),
                                    ALU.subtract).then_inc(w_lo_done.sem, 1)

    def vector_body(dve, pn, p0, p1, p2):
        by_graph = "p (g c) h -> p g c h"
        s_of = sd[:, :, 0:AH]
        d_of = sd[:, :, AH:2 * AH]
        d4 = d_of.rearrange(by_graph, c=2)
        D4 = dmax[:, :].rearrange("p (g h) -> p g h", g=2).unsqueeze(2).broadcast_to([P, 2, 2, AH])
        if pn is not None:
            chain_d0.start(pn)
        if p1 is not None:
            chain_d1.start(p1)
        if p2 is not None:
            chain_d2.start(p2)

        def neighbours(n, p):
            g, head = gat(n)
            dve.wait_ge(use1.sem, use1.upto(p, filled("SR", n)))
            if n >= 2:
                dve.wait_ge(mm_done.sem, mm_done.upto(p, n - 1))
            elif due(p - 1, UNITS):
                dve.wait_ge(mm_done.sem, mm_done.upto(p - 1, UNITS))
            o = bank_of("SR", n)
            for k in range(2):
                for j in range(2):
                    t = 2 * g + j
                    last = nc.vector.scalar_tensor_tensor(
                        Mp[:, n % 2, k, j, :], o[:, k * NODES:(k + 1) * NODES], d_neg[:, t, head + k:head + k + 1],
                        adj_n[:, t, :], ALU.is_ge, ALU.mult)
            last.then_inc(m_done.sem, 1)

        def acc_leave(q, p):
            g, hf = q // 2, q % 2
            heads = slice(hf * NH, (hf + 1) * NH)
            dve.wait_ge(mm_done.sem, mm_done.upto(p, 3 * q + 3))
            if q == 0:
                dve.wait_ge(aneg_done.sem, aneg_done.upto(p, 1))
            if q > 0:
                dve.wait_ge(f_done.sem, f_done.upto(p, 2 * q))
            elif due(p - 1, 2 * T):
                dve.wait_ge(f_done.sem, f_done.upto(p - 1, 2 * T))
            for i in range(2):
                t = 2 * g + i
                left, right = acc[i][:, 0:NH * E1], acc[i][:, NH * E1:2 * NH * E1]
                nc.vector.tensor_tensor(part1[:, i, :, :], left.rearrange("p (h e) -> p h e", h=NH),
                                        a_neg[:, t, heads].unsqueeze(2).broadcast_to([P, NH, E1]), ALU.mult)
                nc.vector.tensor_tensor(part2[:, i, :, :], right.rearrange("p (h e) -> p h e", h=NH),
                                        e_out[:, t, 1, heads].unsqueeze(2).broadcast_to([P, NH, E1]),
                                        ALU.mult).then_inc(acc_out.sem, 1)

        def divide(q, p, chain):
            g, hf = q // 2, q % 2
            heads = slice(hf * NH, (hf + 1) * NH)
            for i in range(2):
                dve.wait_ge(num_done.sem, num_done.upto(p, 2 * q + i + 1))
                last = nc.vector.reciprocal(dinv[:, i, :], part1[:, i, :, OD])
            chain.link(dve, last, p)
            for i in range(2):
                nc.vector.tensor_tensor(h1[:, 2 * g + i, heads, :], part1[:, i, :, 0:OD],
                                        dinv[:, i, :].unsqueeze(2).broadcast_to([P, NH, OD]),
                                        ALU.mult).then_inc(f_done.sem, 1)

        def elu(t):
            dve.wait_ge(e1_done.sem, e1_done.upto(p2, t + 1))
            v = h1[:, t, :, :].rearrange("p h e -> p (h e)")
            nc.vector.scalar_tensor_tensor(v, e_sb[:, t % 2, :], -1.0, v, ALU.add, ALU.max).then_inc(elu_done.sem, 1)

        def mix(tiles):
            for t in tiles:
                dve.wait_ge(w1_done.sem, w1_done.upto(p2, t + 1))
                dve.wait_ge(gate_done.sem, gate_done.upto(p2, t + 1))
                v = h1[:, t, :, :].rearrange("p h e -> p (h e)")
                last = nc.vector.scalar_tensor_tensor(v, gl[:, t, :], 1.0, v, ALU.add, ALU.mult)
            chain_d2.link(dve, last, p2)
            for t in tiles:
                v = h1[:, t, :, :].rearrange("p h e -> p (h e)")
                nc.vector.scalar_tensor_tensor(hy[:, t, :], v, 0.5, hy[:, t, :], ALU.mult, ALU.add).then_inc(out_done.sem, 1)

        def context_low(c):
            dve.wait_ge(pv_done.sem, pv_done.upto(p0, 4 * c + 4))
            dve.wait_ge(chi_done.sem, chi_done.upto(p0, c + 1))
            nc.vector.scalar_tensor_tensor(cT_lo[:, c, :], ctx[:, :], bv_c[:, c:c + 1], cT_hi[:, c, :].bitcast(F32),
                                           ALU.add, ALU.subtract).then_inc(clo_done.sem, 1)

        if p0 is not None:
            for c in range(KC):
                dve.wait_ge(use0.sem, use0.upto(p0, filled("A", c)))
                o = bank_of("A", c)
                dve.wait_ge(hi_done.sem, hi_done.upto(p0, c + 1))
                nc.vector.scalar_tensor_tensor(hT_lo[:, c, :], o[:, :], 0.0, hT_hi[:, c, :].bitcast(F32),
                                               ALU.max, ALU.subtract).then_inc(lo_done.sem, 1)
        if p2 is not None:
            neighbours(EARLY + 1, p2)
        for slot in range(SLOTS + 1):
            if p1 is not None and slot == STATS_SLOT:
                dve.wait_ge(y_done.sem, y_done.upto(p1, T))
                for t in range(T):
                    last = nc.vector.bn_stats(stats2[:, t, :], y[:, t, :])
                chain_d1.link(dve, last, p1)
                settle(dve)
                for t in range(T):
                    last = nc.vector.bn_aggr(mv2[:, t, :], stats2[:, t, :])
                last.then_inc(stat2_done.sem, 1)
            for q in at(LEAVE, STEPS + 1 + slot) if p2 is not None else ():
                acc_leave(q, p2)
            for q in at(DIVIDE, STEPS + 1 + slot) if p2 is not None else ():
                divide(q, p2, chain_d2)
            if p2 is not None and EARLY + 2 + slot < UNITS:
                neighbours(EARLY + 2 + slot, p2)
            for g in at(ELU_SLOTS, slot) if p2 is not None else ():
                elu(2 * g)
                elu(2 * g + 1)
            if p2 is not None and slot == MIX_SLOT:
                mix((0, 1))
            if p1 is not None and slot == ADJ_SLOT:
                dve.wait_ge(adjT_in.sem, adjT_in.upto(p1, 16))
                nc.vector.tensor_scalar(adj_n[:, :, :], adjT_u[:, :, :], -1.0, None, ALU.mult).then_inc(adjN_done.sem, 1)
            if isinstance(p0, int) and p0 == 0 and slot == 3:
                weights_low(3, len(w_names))
            if pn is not None and slot == NEXT_SLOT:
                dve.wait_ge(x_in.sem, x_in.upto(pn, 16))
                for t in range(T):
                    last = nc.vector.bn_stats(stats[:, t, :], x_sb[:, t, :])
                chain_d0.link(dve, last, pn)
                settle(dve)
                for t in range(T):
                    last = nc.vector.bn_aggr(mv[:, t, :], stats[:, t, :])
                last.then_inc(stat_done.sem, 1)
        if p1 is not None:
            for c in range(KC):
                dve.wait_ge(e_filled.sem, e_filled.upto(p1, c + 1))
                o = bank_of("E", c)
                dve.wait_ge(hi2_done.sem, hi2_done.upto(p1, c + 1))
                nc.vector.scalar_tensor_tensor(hT_lo[:, c, :], o[:, :], 0.0, hT_hi[:, c, :].bitcast(F32),
                                               ALU.max, ALU.subtract).then_inc(lo2_done.sem, 1)
        if p2 is not None:
            mix((2, 3))
        for s in range(STEPS):
            for q in at(LEAVE, s) if p1 is not None else ():
                acc_leave(q, p1)
            if p0 is not None and 0 <= s - 1 < UNITS:
                n = s - 1
                dve.wait_ge(exp_done.sem, exp_done.upto(p0, 2 * n + 2))
                nc.vector.reciprocal(rinv[:, n % 4, :], rsum[:, n % 4, :]).then_inc(rinv_done.sem, 1)
            if p0 is not None and s < UNITS:
                dve.wait_ge(use0.sem, use0.upto(p0, filled("S", s)))
                o = bank_of("S", s)
                nc.vector.tensor_reduce(nmax[:, s % 4, :], o[:, :].rearrange("p (q k) -> p q k", q=2),
                                        AX.X, ALU.max, negate=True).then_inc(max_done.sem, 1)
            if p0 is not None and 0 <= s - 1 < UNITS:
                n = s - 1
                dve.wait_ge(rinv_done.sem, rinv_done.upto(p0, n + 1))
                nc.vector.tensor_scalar(probs[:, n % 4, 1, :], probs[:, n % 4, 1, :], rinv[:, n % 4, 1:2], None,
                                        ALU.mult).then_inc(pn1_done.sem, 1)
            for t in at(GATE_STEPS, s) if p1 is not None else ():
                dve.wait_ge(use1.sem, use1.upto(p1, filled("gate", t)))
                o = bank_of("gate", t)
                nc.vector.tensor_tensor(gl[:, t, :], o[:, 0:H], Hb_b[:, :], ALU.add).then_inc(gl_done.sem, 1)
            for t in at(SD_STEPS, s) if p1 is not None else ():
                dve.wait_ge(tw_done.sem, tw_done.upto(p1, t + 1))
                nc.vector.tensor_reduce(sd[:, t, :], tw[:, t % 2, :, :], AX.X, ALU.add).then_inc(sd_done.sem, 1)
            if p1 is not None and s == PREPARE:
                dve.wait_ge(sd_done.sem, sd_done.upto(p1, T))
                nc.vector.tensor_tensor(dmax2[:, :].rearrange("p (g h) -> p g h", g=2), d4[:, :, 0, :],
                                        d4[:, :, 1, :], ALU.max).then_inc(dm_done.sem, 1)
                sp3 = s_parts[:, :, :].rearrange("p t (j h) -> p t j h", j=3)
                chain_d1.link(dve, nc.vector.tensor_copy(sp3[:, :, 0, :], s_of), p1)
                chain_d1.link(dve, nc.vector.tensor_tensor(s_rest[:, :, :], s_of, sp3[:, :, 0, :], ALU.subtract), p1)
                chain_d1.link(dve, nc.vector.tensor_copy(sp3[:, :, 1, :], s_rest[:, :, :]), p1)
                nc.vector.tensor_tensor(sp3[:, :, 2, :], s_rest[:, :, :], sp3[:, :, 1, :], ALU.subtract).then_inc(parts_done.sem, 1)
                nc.vector.tensor_scalar(d_neg[:, :, :], d_of, -1.0, None, ALU.mult).then_inc(dneg_done.sem, 1)
            if p1 is not None and s == PREPARE + 1:
                dve.wait_ge(dmax_done.sem, dmax_done.upto(p1, 1))
                chain_d1.link(dve, nc.vector.tensor_tensor(u_sb[:, :, :].rearrange(by_graph, c=2),
                                                           s_of.rearrange(by_graph, c=2), D4, ALU.add), p1)
                chain_d1.link(dve, nc.vector.scalar_tensor_tensor(m_sb[:, :, :], u_sb[:, :, :], LEAK, u_sb[:, :, :],
                                                                  ALU.mult, ALU.max), p1)
                nc.vector.tensor_tensor(e_in[:, :, 0, :], u_sb[:, :, :], m_sb[:, :, :], ALU.subtract)
                nc.vector.scalar_tensor_tensor(e_in[:, :, 1, :], u_sb[:, :, :], LEAK, m_sb[:, :, :], ALU.mult, ALU.subtract)
                nc.vector.tensor_tensor(e_in[:, :, 2, :].rearrange(by_graph, c=2), d4, D4, ALU.subtract).then_inc(ein_done.sem, 1)
            if p1 is not None and s == FACTORS[0]:
                dve.wait_ge(e_done.sem, e_done.upto(p1, 2))
                nc.vector.tensor_scalar(a_neg[:, :, :], e_out[:, :, 0, :], -1.0, None, ALU.mult).then_inc(aneg_done.sem, 1)
            if p1 is not None and s in FACTORS:
                t = FACTORS.index(s)
                if t >= 2:
                    dve.wait_ge(x2_done.sem, x2_done.upto(p1, t - 1))
                dve.wait_ge(h1_done.sem, h1_done.upto(p1, t + 1))
                nc.vector.tensor_tensor(G[:, t % 2, 0, :, 0:OD], h1[:, t, :, :],
                                        e_out[:, t, 2, :].unsqueeze(2).broadcast_to([P, AH, OD]), ALU.mult)
                nc.vector.tensor_copy(G[:, t % 2, 0, :, OD:E1], e_out[:, t, 2, :].unsqueeze(2))
                nc.vector.tensor_copy(G[:, t % 2, 1, :, OD:E1], e_leak[:, t, :].unsqueeze(2)).then_inc(g1_done.sem, 1)
            if p1 is not None and 0 <= s - FIRST < EARLY:
                if s == FIRST:
                    dve.wait_ge(dneg_done.sem, dneg_done.upto(p1, 1))
                    dve.wait_ge(adjN_done.sem, adjN_done.upto(p1, 1))
                neighbours(s - FIRST, p1)
            if p1 is not None and s - 1 in FACTORS:
                t = FACTORS.index(s - 1)
                dve.wait_ge(x0_done.sem, x0_done.upto(p1, t + 1))
                flat = "p r h e -> p (r h e)"
                nc.vector.tensor_tensor(G[:, t % 2, :, :, :].rearrange(flat), G[:, t % 2, :, :, :].rearrange(flat),
                                        X[:, t, 0, :, :, :].rearrange(flat), ALU.subtract).then_inc(r_done.sem, 1)
            if p0 is not None and s in CONTEXT:
                context_low(CONTEXT.index(s))
            for q in at(DIVIDE, s) if p1 is not None else ():
                divide(q, p1, chain_d1)
        if p1 is not None and (EARLY - 1) % 3 == 0:
            acc_leave((EARLY - 1) // 3 - 1, p1)
        if p0 is not None:
            context_low(KC - 1)
        if p1 is not None and EARLY % 3 == 0:
            acc_leave(EARLY // 3 - 1, p1)
        for t in range(T):
            if p1 is not None and t == 3:
                neighbours(EARLY, p1)
            if p0 is not None:
                dve.wait_ge(use0.sem, use0.upto(p0, filled("D", t)))
                o = bank_of("D", t)
                if t == 0:
                    dve.wait_ge(xb_done.sem, xb_done.upto(p0, 1))
                if t == 0 and due(p0 - 1, T):
                    dve.wait_ge(hy_done.sem, hy_done.upto(p0 - 1, T))
                nc.vector.tensor_tensor(y[:, t, :], o[:, 0:H], xb[:, t, :], ALU.add).then_inc(y_done.sem, 1)

    def weights_high(first, end):
        for n in range(first, end):
            nc.scalar.wait_ge(w_in[n].sem, 16)
            nc.scalar.activation(w_hi[w_names[n]][:, :, :], stage[n], ACT.Copy).then_inc(w_hi_done.sem, 1)

    def scalar_body(act, pn, p0, p1, p2):
        flat = "p h e -> p (h e)"
        flat4 = "p r h e -> p (r h e)"
        if p2 is not None:
            chain_a2.start(p2)

        def context_high(c):
            act.wait_ge(pv_done.sem, pv_done.upto(p0, 4 * c + 4))
            nc.scalar.activation(cT_hi[:, c, :], ctx[:, :], ACT.Identity, bias=bv_c[:, c:c + 1]).then_inc(chi_done.sem, 1)

        if p0 is not None:
            for c in range(KC):
                act.wait_ge(use0.sem, use0.upto(p0, filled("A", c)))
                o = bank_of("A", c)
                nc.scalar.activation(hT_hi[:, c, :], o[:, :], ACT.Relu).then_inc(hi_done.sem, 1)
        for slot in range(SLOTS + 1):
            if p2 is not None and slot in EXP_SLOTS:
                g = EXP_SLOTS.index(slot)
                tiles = (2 * g, 2 * g + 1)
                for t in tiles:
                    act.wait_ge(v1_done.sem, v1_done.upto(p2, t + 1))
                    if t >= 2:
                        act.wait_ge(elu_done.sem, elu_done.upto(p2, t - 1))
                    elif due(p2 - 1, T):
                        act.wait_ge(elu_done.sem, elu_done.upto(p2 - 1, T))
                    last = nc.scalar.activation(e_sb[:, t % 2, :], h1[:, t, :, :].rearrange(flat), ACT.Relu, scale=-1.0)
                chain_a2.link(act, last, p2)
                for t in tiles:
                    nc.scalar.activation(e_sb[:, t % 2, :], e_sb[:, t % 2, :], ACT.Exp, scale=-1.0).then_inc(e1_done.sem, 1)
            if isinstance(p0, int) and p0 == 0 and slot == 3:
                weights_high(3, len(w_names))
            if p1 is not None and slot == NORM_SLOT:
                act.wait_ge(rstd2_done.sem, rstd2_done.upto(p1, 1))
                if p0 is not None:
                    act.wait_ge(use0.sem, use0.upto(p0, filled("A", KC - 1)))
                for t in range(T):
                    nc.scalar.activation(hn[:, t, :], y[:, t, :], ACT.Identity, scale=rstd2[:, t:t + 1],
                                         bias=shift2[:, t:t + 1]).then_inc(ln2_done.sem, 1)
            if p0 is not None and 0 <= slot - 1 < SLOTS:
                what, k = PROJECTIONS[slot - 1]
                act.wait_ge(use0.sem, use0.upto(p0, filled(what, k)))
                o = bank_of(what, k)
                if what == "Q":
                    nc.scalar.activation(qT[:, k, :], o[:, :], ACT.Identity, bias=bq8_c[:, k:k + 1],
                                         scale=float(HD) ** -0.5).then_inc(q_done.sem, 1)
                elif what == "K":
                    nc.scalar.activation(kT[:, k, :], o[:, :], ACT.Identity, bias=bk_c[:, k:k + 1]).then_inc(k_done.sem, 1)
                else:
                    nc.scalar.activation(v_sb[:, k, :], o[:, 0:H], ACT.Copy).then_inc(v_done.sem, 1)
            if p1 is not None and slot == ADJ_SLOT:
                act.wait_ge(adjT_in.sem, adjT_in.upto(p1, 16))
                if due(p1 - 1, UNITS):
                    act.wait_ge(mm_done.sem, mm_done.upto(p1 - 1, UNITS))
                nc.scalar.activation(adj_p[:, :, :], adjT_u[:, :, :], ACT.Copy).then_inc(adjT_done.sem, 1)
        if p1 is not None:
            for c in range(KC):
                act.wait_ge(e_filled.sem, e_filled.upto(p1, c + 1))
                o = bank_of("E", c)
                nc.scalar.activation(hT_hi[:, c, :], o[:, :], ACT.Relu).then_inc(hi2_done.sem, 1)
        for s in range(STEPS):
            if p0 is not None and s in CONTEXT:
                context_high(CONTEXT.index(s))
            for t in at(GATE_STEPS, s - 1) if p1 is not None else ():
                act.wait_ge(gl_done.sem, gl_done.upto(p1, t + 1))
                nc.scalar.activation(gl[:, t, :], gl[:, t, :], ACT.Tanh, scale=0.5).then_inc(gate_done.sem, 1)
            if p0 is not None and 0 <= s - 1 < UNITS:
                n = s - 1
                act.wait_ge(rinv_done.sem, rinv_done.upto(p0, n + 1))
                nc.scalar.activation(probs[:, n % 4, 0, :], probs[:, n % 4, 0, :], ACT.Copy,
                                     scale=rinv[:, n % 4, 0:1]).then_inc(pn0_done.sem, 1)
            if p0 is not None and s < UNITS:
                o = bank_of("S", s)
                act.wait_ge(max_done.sem, max_done.upto(p0, s + 1))
                if s >= 4:
                    act.wait_ge(use0.sem, use0.upto(p0, filled("PT", s - 4)))
                elif due(p0 - 1, 1):
                    act.wait_ge(use0.sem, use0.upto(p0 - 1, filled("PT", UNITS - 1)))
                for q in range(2):
                    nc.scalar.activation(probs[:, s % 4, q, :], o[:, q * NODES:(q + 1) * NODES], ACT.Exp,
                                         bias=nmax[:, s % 4, q:q + 1],
                                         accum_out=rsum[:, s % 4, q:q + 1]).then_inc(exp_done.sem, 1)
            for t in at(H_STEPS, s) if p1 is not None else ():
                act.wait_ge(use1.sem, use1.upto(p1, filled("h", t)))
                o = bank_of("h", t)
                if t == 0 and due(p1 - 1, T):
                    act.wait_ge(elu_done.sem, elu_done.upto(p1 - 1, T))
                if t >= 2:
                    act.wait_ge(tw_done.sem, tw_done.upto(p1, t - 1))
                nc.scalar.activation(th[:, t % 2, :, :].rearrange(flat), o[:, 0:H], ACT.Tanh).then_inc(th_done.sem, 1)
                if t == 0 and due(p1 - 1, T):
                    act.wait_ge(out_done.sem, out_done.upto(p1 - 1, T))
                nc.scalar.activation(h1[:, t, :, :].rearrange(flat), o[:, 0:H], ACT.Copy).then_inc(h1_done.sem, 1)
            if p0 is not None and 0 <= s - 2 < UNITS:
                n = s - 2
                act.wait_ge(use0.sem, use0.upto(p0, filled("PT", n)))
                o = bank_of("PT", n)
                if n >= 3:
                    act.wait_ge(pv_done.sem, pv_done.upto(p0, n - 2))
                elif due(p0 - 1, UNITS):
                    act.wait_ge(pv_done.sem, pv_done.upto(p0 - 1, UNITS))
                nc.scalar.activation(probsT[:, n % 3, :, :].rearrange("p k q -> p (k q)"), o[:, :], ACT.Copy).then_inc(pt_done.sem, 1)
            if p1 is not None and s == PREPARE + 1:
                act.wait_ge(ein_done.sem, ein_done.upto(p1, 1))
                nc.scalar.activation(e_out[:, :, 0:2, :], e_in[:, :, 0:2, :], ACT.Exp)
                nc.scalar.activation(e_out[:, :, 2, :], e_in[:, :, 2, :], ACT.Exp, bias=shift_c[:, :]).then_inc(e_done.sem, 1)
                nc.scalar.activation(e_leak[:, :, :], e_in[:, :, 2, :], ACT.Exp, scale=LEAK, bias=shift_c[:, :]).then_inc(e_done.sem, 1)
            if p1 is not None and s - MIDDLE in FACTORS:
                t = FACTORS.index(s - MIDDLE)
                act.wait_ge(r_done.sem, r_done.upto(p1, t + 1))
                nc.scalar.activation(X[:, t, 1, :, :, :].rearrange(flat4), G[:, t % 2, :, :, :].rearrange(flat4),
                                     ACT.Copy).then_inc(x1_done.sem, 1)
            if p1 is not None and s in FACTORS:
                t = FACTORS.index(s)
                act.wait_ge(g1_done.sem, g1_done.upto(p1, t + 1))
                act.wait_ge(g2_done.sem, g2_done.upto(p1, t + 1))
                nc.scalar.activation(X[:, t, 0, :, :, :].rearrange(flat4), G[:, t % 2, :, :, :].rearrange(flat4),
                                     ACT.Copy).then_inc(x0_done.sem, 1)
            if p1 is not None and s == S_STEP:
                act.wait_ge(use1.sem, use1.upto(p1, filled("sT", 0)))
                o = bank_of("sT", 0)
                nc.scalar.activation(sT[0:3 * AH, :], o[:, :].bitcast(BF16)[0:3 * AH, 0:W], ACT.Copy).then_inc(sT_done.sem, 1)
            if pn is not None and s == NORM:
                act.wait_ge(rstd_done.sem, rstd_done.upto(pn, 1))
                if p1 is not None:
                    act.wait_ge(e_filled.sem, e_filled.upto(p1, KC))
                elif p0 is not None:
                    act.wait_ge(use0.sem, use0.upto(p0, filled("A", KC - 1)))
                for t in range(T):
                    nc.scalar.activation(hn[:, t, :], x_sb[:, t, :], ACT.Identity, scale=rstd[:, t:t + 1],
                                         bias=shift1[:, t:t + 1]).then_inc(ln1_done.sem, 1)
            if p1 is not None and s < 2:
                if s == 0:
                    act.wait_ge(ln2_done.sem, ln2_done.upto(p1, T))
                for t in (2 * s, 2 * s + 1):
                    nc.scalar.activation(hr[:, t, :], hn[:, t, :], ACT.Relu).then_inc(hr_done.sem, 1)
        if p0 is not None:
            context_high(KC - 1)

    def gpsimd_body(pool, pn, p0, p1, p2):
        flat = "p h e -> p (h e)"
        if pn is not None:
            chain_p0.start(pn)
        if p1 is not None:
            chain_p1.start(p1)

        def sum_parts(q, p):
            for i in range(2):
                pool.wait_ge(acc_out.sem, acc_out.upto(p, 2 * q + i + 1))
                nc.gpsimd.tensor_tensor(part1[:, i, :, :].rearrange(flat), part1[:, i, :, :].rearrange(flat),
                                        part2[:, i, :, :].rearrange(flat), ALU.add).then_inc(num_done.sem, 1)

        def add_bias(g, p):
            for t in (2 * g, 2 * g + 1):
                pool.wait_ge(f_done.sem, f_done.upto(p, 4 * g + 2 + t % 2 + 1))
                nc.gpsimd.tensor_tensor(h1[:, t, :, :], h1[:, t, :, :],
                                        gb_b[:, :].unsqueeze(1).broadcast_to([P, AH, OD]), ALU.add).then_inc(v1_done.sem, 1)

        for slot in range(SLOTS + 1):
            for q in at(LEAVE, STEPS + 1 + slot) if p2 is not None else ():
                sum_parts(q, p2)
            if p0 is not None and slot == 0:
                pool.wait_ge(adj_in.sem, adj_in.upto(p0, 16))
                if due(p0 - 1, 1):
                    pool.wait_ge(use0.sem, use0.upto(p0 - 1, filled("S", UNITS - 1)))
                settle(pool)
                nc.gpsimd.tensor_scalar(mask[:, :, :], adj_u[:, :, :], -MASKED, MASKED, ALU.mult, ALU.add).then_inc(mask_done.sem, 1)
            if p1 is not None and slot == STATS_SLOT:
                pool.wait_ge(stat2_done.sem, stat2_done.upto(p1, 1))
                settle(pool)
                nc.gpsimd.tensor_scalar(negmean2[:, :], mv2[:, :, 0], -1.0, None, ALU.mult)
                chain_p1.link(pool, nc.gpsimd.tensor_scalar(veps2[:, :], mv2[:, :, 1], EPS, None, ALU.add), p1)
                chain_p1.link(pool, nc.gpsimd.tensor_tensor(rstd2[:, :], veps2[:, :], half[:, 0:T], ALU.pow), p1)
                nc.gpsimd.tensor_tensor(shift2[:, :], negmean2[:, :], rstd2[:, :], ALU.mult).then_inc(rstd2_done.sem, 1)
            for g in at(ELU_SLOTS, slot) if p2 is not None else ():
                for t in (2 * g, 2 * g + 1):
                    pool.wait_ge(elu_done.sem, elu_done.upto(p2, t + 1))
                    v = h1[:, t, :, :].rearrange(flat)
                    nc.gpsimd.tensor_tensor(v, v, hr[:, t, :], ALU.subtract).then_inc(w1_done.sem, 1)
            if p0 is not None and slot == 2:
                if due(p0 - 1, T):
                    pool.wait_ge(y_done.sem, y_done.upto(p0 - 1, T))
                pool.wait_ge(x_in.sem, x_in.upto(p0, 16))
                for t in range(T):
                    last = nc.gpsimd.tensor_tensor(xb[:, t, :], x_sb[:, t, :], bf_b[:, :], ALU.add)
                last.then_inc(xb_done.sem, 1)
            for q in at(DIVIDE, STEPS + 1 + slot) if p2 is not None else ():
                if q % 2:
                    add_bias(q // 2, p2)

        if pn is not None:
            pool.wait_ge(stat_done.sem, stat_done.upto(pn, 1))
            settle(pool)
            nc.gpsimd.tensor_scalar(negmean[:, :], mv[:, :, 0], -1.0, None, ALU.mult)
            chain_p0.link(pool, nc.gpsimd.tensor_scalar(veps[:, :], mv[:, :, 1], EPS, None, ALU.add), pn)
            chain_p0.link(pool, nc.gpsimd.tensor_tensor(rstd[:, :], veps[:, :], half[:, 0:T], ALU.pow), pn)
            nc.gpsimd.tensor_tensor(shift1[:, :], negmean[:, :], rstd[:, :], ALU.mult).then_inc(rstd_done.sem, 1)
        for s in range(STEPS):
            if p1 is not None and s == HY_STEP:
                pool.wait_ge(hr_done.sem, hr_done.upto(p1, T))
                for g in range(2):
                    if due(p1 - 1, 16):
                        pool.wait_ge(stored[g].sem, stored[g].upto(p1 - 1, 16))
                for t in range(T):
                    nc.gpsimd.tensor_tensor(hy[:, t, :], hr[:, t, :], y[:, t, :], ALU.add).then_inc(hy_done.sem, 1)
            if p1 is not None and s == PREPARE:
                pool.wait_ge(dm_done.sem, dm_done.upto(p1, 1))
                settle(pool)
                nc.gpsimd.partition_all_reduce(dmax[:, :], dmax2[:, :], P, bass.bass_isa.ReduceOp.max).then_inc(dmax_done.sem, 1)
            if p1 is not None and s - MIDDLE in FACTORS:
                t = FACTORS.index(s - MIDDLE)
                f3 = "p r h e -> p (r h e)"
                pool.wait_ge(x1_done.sem, x1_done.upto(p1, t + 1))
                nc.gpsimd.tensor_tensor(X[:, t, 2, :, :, :].rearrange(f3), G[:, t % 2, :, :, :].rearrange(f3),
                                        X[:, t, 1, :, :, :].rearrange(f3), ALU.subtract).then_inc(x2_done.sem, 1)
            if p1 is not None and s in FACTORS:
                t = FACTORS.index(s)
                pool.wait_ge(e_done.sem, e_done.upto(p1, 2))
                pool.wait_ge(h1_done.sem, h1_done.upto(p1, t + 1))
                if t >= 2:
                    pool.wait_ge(x2_done.sem, x2_done.upto(p1, t - 1))
                nc.gpsimd.tensor_tensor(G[:, t % 2, 1, :, 0:OD], h1[:, t, :, :],
                                        e_leak[:, t, :].unsqueeze(2).broadcast_to([P, AH, OD]), ALU.mult).then_inc(g2_done.sem, 1)
            for t in at(H_STEPS, s) if p1 is not None else ():
                pool.wait_ge(th_done.sem, th_done.upto(p1, t + 1))
                if t == 0 and due(p1 - 1, T):
                    pool.wait_ge(x2_done.sem, x2_done.upto(p1 - 1, T))
                if t >= 2:
                    pool.wait_ge(sd_done.sem, sd_done.upto(p1, t - 1))
                th_f = th[:, t % 2, :, :].rearrange(flat)
                nc.gpsimd.tensor_tensor(tw[:, t % 2, 0:AH, :].rearrange(flat), th_f, wsrc_b[:, :], ALU.mult)
                nc.gpsimd.tensor_tensor(tw[:, t % 2, AH:2 * AH, :].rearrange(flat), th_f,
                                        wdst_b[:, :], ALU.mult).then_inc(tw_done.sem, 1)
            for q in at(LEAVE, s) if p1 is not None else ():
                sum_parts(q, p1)
        for q in at(LEAVE, STEPS) if p1 is not None else ():
            sum_parts(q, p1)

    shift_c = sb("shift_c", [P, 1])
    block = nc.Block()
    with block:
        @block.sync
        def _(sp):
            sp.dma_start(x_sb[:, :, :], x_v[0, :, :, :]).then_inc(x_in.sem, 16)
            sp.dma_start(adj_u[:, :, :], adj_v[0, :, :, :]).then_inc(adj_in.sem, 16)
            sp.dma_start(stage[0], w_dram[0].rearrange("(c p) n -> p c n", p=P)).then_inc(w_in[0].sem, 16)
            for col, dst in ((bq, bq_c), (bk, bk_c), (bv, bv_c)):
                sp.dma_start(dst[:, :], col).then_inc(rows_in.sem, 16)
            for row, dst in ((bf, bf_b), (Hb, Hb_b), (w_src, wsrc_b), (w_dst, wdst_b), (gb, gb_b)):
                sp.dma_start(dst[:, :], row.partition_broadcast(P).rearrange("p a n -> p (a n)")).then_inc(rows_in.sem, 16)
            for n in range(1, len(w_names)):
                sp.dma_start(stage[n], w_dram[n].rearrange("(c p) n -> p c n", p=P)).then_inc(w_in[n].sem, 16)
            sync_body(sp, 1, 0, None, None)
            sync_body(sp, 2, 1, 0, None)
            sync_body(sp, 3, 2, 1, 0)
            with sp.Fori(3, PAIRS - 1) as i:
                sync_body(sp, i + 1, i, i - 1, i - 2)
            sync_body(sp, None, PAIRS - 1, PAIRS - 2, PAIRS - 3)
            sync_body(sp, None, None, PAIRS - 1, PAIRS - 2)
            sync_body(sp, None, None, None, PAIRS - 1)
            for g in range(2):
                sp.wait_ge(stored[g].sem, stored[g].upto(PAIRS, 0))

        @block.tensor
        def _(pe):
            pe.wait_ge(consts.sem, 3)
            tensor_body(pe, 0, None, None)
            pe.wait_ge(sel_done, 1)
            tensor_body(pe, 1, 0, None)
            tensor_body(pe, 2, 1, 0)
            with pe.Fori(3, PAIRS) as i:
                tensor_body(pe, i, i - 1, i - 2)
            tensor_body(pe, None, PAIRS - 1, PAIRS - 2)
            tensor_body(pe, None, None, PAIRS - 1)

        @block.vector
        def _(dve):
            nc.vector.memset(shift_c[:, :], SHIFT).then_inc(consts.sem, 1)
            vector_body(dve, 0, None, None, None)
            dve.wait_ge(rows_in.sem, 16 * 8)
            nc.vector.tensor_scalar(bq8_c[:, :], bq_c[:, :], float(HD) ** -0.5, None, ALU.mult).then_inc(consts.sem, 1)
            weights_low(0, 3)
            vector_body(dve, 1, 0, None, None)
            vector_body(dve, 2, 1, 0, None)
            vector_body(dve, 3, 2, 1, 0)
            with dve.Fori(3, PAIRS - 1) as i:
                vector_body(dve, i + 1, i, i - 1, i - 2)
            vector_body(dve, None, PAIRS - 1, PAIRS - 2, PAIRS - 3)
            vector_body(dve, None, None, PAIRS - 1, PAIRS - 2)
            vector_body(dve, None, None, None, PAIRS - 1)

        @block.scalar
        def _(act):
            scalar_body(act, 0, None, None, None)
            weights_high(0, 3)
            act.wait_ge(rows_in.sem, 16 * 8)
            act.wait_ge(consts.sem, 3)
            scalar_body(act, 1, 0, None, None)
            scalar_body(act, 2, 1, 0, None)
            scalar_body(act, 3, 2, 1, 0)
            with act.Fori(3, PAIRS - 1) as i:
                scalar_body(act, i + 1, i, i - 1, i - 2)
            scalar_body(act, None, PAIRS - 1, PAIRS - 2, PAIRS - 3)
            scalar_body(act, None, None, PAIRS - 1, PAIRS - 2)
            scalar_body(act, None, None, None, PAIRS - 1)

        @block.gpsimd
        def _(pool):
            set_up = nc.alloc_semaphore("set_up")
            nc.gpsimd.memset(half[:, :], -0.5).then_inc(set_up, 1)
            nc.gpsimd.memset(ident[:, :], 0.0).then_inc(set_up, 1)
            nc.gpsimd.memset(sel[:, :, :], 0.0).then_inc(set_up, 1)
            nc.gpsimd.memset(sT[:, :], 0.0).then_inc(set_up, 1)
            pool.wait_ge(set_up, 4)
            nc.gpsimd.affine_select(out=ident[:, :], in_=ident[:, :], compare_op=ALU.not_equal, fill=1.0, base=0,
                                    pattern=[[-1, P]], channel_multiplier=1).then_inc(set_up, 1)
            pool.wait_ge(set_up, 5)
            nc.gpsimd.tensor_copy(ident_b[:, :], ident[:, :]).then_inc(set_up, 1)
            pool.wait_ge(set_up, 6)
            pool.nop().then_inc(consts.sem, 1)
            gpsimd_body(pool, 0, None, None, None)
            for j in range(3):
                nc.gpsimd.affine_select(out=sel[:, :, :], in_=sel[:, :, :], compare_op=ALU.not_equal, fill=1.0,
                                        base=-AH * j, pattern=[[-1, AH], [0, P]], channel_multiplier=1).then_inc(set_up, 1)
                pool.wait_ge(set_up, 7 + j)
            pool.wait_ge(rows_in.sem, 16 * 8)
            pool.nop().then_inc(sel_done, 1)
            gpsimd_body(pool, 1, 0, None, None)
            gpsimd_body(pool, 2, 1, 0, None)
            gpsimd_body(pool, 3, 2, 1, 0)
            with pool.Fori(3, PAIRS - 1) as i:
                gpsimd_body(pool, i + 1, i, i - 1, i - 2)
            gpsimd_body(pool, None, PAIRS - 1, PAIRS - 2, PAIRS - 3)
            gpsimd_body(pool, None, None, PAIRS - 1, PAIRS - 2)
            gpsimd_body(pool, None, None, None, PAIRS - 1)


_INS = ["x", "adj", "adjT", "Wq", "Wk", "Wv", "Wf", "W1", "HwT", "bq", "bk", "bv", "bf", "gb", "w_src", "w_dst", "Hb"]


def kernel(**inputs):
    import numpy as np
    import concourse.bacc as bacc
    from concourse.bass_utils import run_bass_kernel_spmd

    a = {k: np.asarray(v) for k, v in inputs.items()}
    adj = a["adj"]
    laid = {
        "x": a["x"], "adj": adj, "adjT": adj.transpose(0, 2, 1),
        "Wq": a["L0_gnn_Wq"], "Wk": a["L0_gnn_Wk"], "Wv": a["L0_gnn_Wv"], "Wf": a["L0_gnn_Wf"],
        "W1": a["L1_gnn_W"].transpose(1, 0, 2).reshape(H, H), "HwT": a["L1_gnn_H_w"].T,
        "bq": a["L0_gnn_bq"].reshape(KC, P).T, "bk": a["L0_gnn_bk"].reshape(KC, P).T, "bv": a["L0_gnn_bv"].reshape(KC, P).T, "bf": a["L0_gnn_bf"][None],
        "gb": a["L1_gnn_b"][None], "w_src": a["L1_gnn_w_src"].reshape(1, H), "w_dst": a["L1_gnn_w_dst"].reshape(1, H),
        "Hb": a["L1_gnn_H_b"][None],
    }
    nc = bacc.Bacc("TRN2", target_bir_lowering=False, num_devices=1)
    arrays, args = {}, []
    for name in _INS:
        v = np.ascontiguousarray(laid[name])
        arrays[f"in_{name}"] = v
        args.append(nc.dram_tensor(f"in_{name}", v.shape, mybir.dt.from_np(v.dtype), kind="ExternalInput").ap())
    args.append(nc.dram_tensor("out", (GRAPHS, NODES, H), F32, kind="ExternalOutput").ap())
    graph_layers(nc, *args)
    r = run_bass_kernel_spmd(nc, [arrays], core_ids=[0])
    return r.results[0]["out"]
```
